# Optimizing a Trainium2 kernel written in Bass

```python
import numpy as np
import jax
import jax.numpy as jnp

def _softmax(x, axis=-1):
    return jax.nn.softmax(x, axis=axis)

def _gelu(x):
    return jax.nn.gelu(x, approximate=True)

def _silu(x):
    return jax.nn.silu(x)

def _sigmoid(x):
    return jax.nn.sigmoid(x)

def _layernorm(x, axis=-1, eps=1e-05):
    m = jnp.mean(x, axis=axis, keepdims=True)
    v = jnp.var(x, axis=axis, keepdims=True)
    return (x - m) / jnp.sqrt(v + eps)

def _scatter_add(tgt, idx, src, axis=0):
    return tgt.at[idx].add(src)

def _segment_sum(src, seg, n):
    return jax.ops.segment_sum(src, seg, n)
kernel_name = 'mk_seq_postln_d1_jaxref_r8_f42381'

def setup_inputs(seed: int=0):
    np.random.seed(seed)
    _w = jnp.asarray

    def _L0_attn_setup():
        import jax, jax.numpy as jnp
        import numpy as np
        HIDDEN = 512
        NUM_HEADS = 32
        HEAD_DIM = HIDDEN // NUM_HEADS

        def _fp8_roundtrip(x):
            return x.astype(jnp.float8_e4m3fn).astype(jnp.float32)
        key = jax.random.key(seed)
        ks = jax.random.split(key, 10)
        B, S = (2, 512)
        hidden_states = jax.random.normal(ks[0], (B, S, HIDDEN), dtype=jnp.float32)
        scale = 0.02

        def lin(kw, kb):
            w = jax.random.normal(kw, (HIDDEN, HIDDEN), dtype=jnp.float32) * scale
            b = jax.random.normal(kb, (HIDDEN,), dtype=jnp.float32) * scale
            return (w, b)
        wq, bq = lin(ks[1], ks[2])
        wk, bk = lin(ks[3], ks[4])
        wv, bv = lin(ks[5], ks[6])
        wl, bl = lin(ks[7], ks[8])
        wq, bq = (_fp8_roundtrip(wq), _fp8_roundtrip(bq))
        wk, bk = (_fp8_roundtrip(wk), _fp8_roundtrip(bk))
        wv, bv = (_fp8_roundtrip(wv), _fp8_roundtrip(bv))
        return {'hidden_states': hidden_states, 'wq': wq, 'bq': bq, 'wk': wk, 'bk': bk, 'wv': wv, 'bv': bv, 'wl': wl, 'bl': bl}
    _L0_attn_in = _L0_attn_setup()

    def _L0_ffn_setup():
        import jax, jax.numpy as jnp
        import numpy as np
        NF4_CODE = jnp.array([-1.0, -0.6961928009986877, -0.5250730514526367, -0.39491748809814453, -0.28444138169288635, -0.18477343022823334, -0.09105003625154495, 0.0, 0.07958029955625534, 0.16093020141124725, 0.24611230194568634, 0.33791524171829224, 0.44070982933044434, 0.5626170039176941, 0.7229568362236023, 1.0], dtype=jnp.float32)
        BLOCKSIZE = 64

        def nf4_quant_dequant(w):
            shape = w.shape
            flat = w.reshape(-1, BLOCKSIZE)
            absmax = jnp.max(jnp.abs(flat), axis=1, keepdims=True)
            normalized = flat / jnp.where(absmax == 0, 1.0, absmax)
            bounds = (NF4_CODE[:-1] + NF4_CODE[1:]) * 0.5
            idx = jnp.searchsorted(bounds, normalized)
            return (NF4_CODE[idx] * absmax).reshape(shape)
        key = jax.random.key(seed)
        k1, k2, k3, kx = jax.random.split(key, 4)
        D, H = (512, 1376)
        scale = 0.02
        w1 = jax.random.normal(k1, (H, D), jnp.float32) * scale
        w2 = jax.random.normal(k2, (H, D), jnp.float32) * scale
        w3 = jax.random.normal(k3, (D, H), jnp.float32) * scale
        x = jax.random.normal(kx, (2, 256, D), jnp.float32)
        return {'x': x, 'w1': w1, 'w2': w2, 'w3': w3}
    _L0_ffn_in = _L0_ffn_setup()
    _d = {'L0_attn_hidden_states': _L0_attn_in['hidden_states'], 'L0_attn_wq': _L0_attn_in['wq'], 'L0_attn_bq': _L0_attn_in['bq'], 'L0_attn_wk': _L0_attn_in['wk'], 'L0_attn_bk': _L0_attn_in['bk'], 'L0_attn_wv': _L0_attn_in['wv'], 'L0_attn_bv': _L0_attn_in['bv'], 'L0_attn_wl': _L0_attn_in['wl'], 'L0_attn_bl': _L0_attn_in['bl'], 'L0_ffn_w1': _L0_ffn_in['w1'], 'L0_ffn_w2': _L0_ffn_in['w2'], 'L0_ffn_w3': _L0_ffn_in['w3']}
    _x0 = _d['L0_attn_hidden_states']
    _d['L0_attn_hidden_states'] = jax.random.normal(jax.random.fold_in(jax.random.key(seed), 1), (4, 512, 512), dtype=_x0.dtype)
    del _x0
    return _d

def reference(L0_attn_hidden_states, L0_attn_wq, L0_attn_bq, L0_attn_wk, L0_attn_bk, L0_attn_wv, L0_attn_bv, L0_attn_wl, L0_attn_bl, L0_ffn_w1, L0_ffn_w2, L0_ffn_w3):

    def _L0_attn_ref(hidden_states, wq, bq, wk, bk, wv, bv, wl, bl):
        import jax, jax.numpy as jnp
        import numpy as np
        HIDDEN = 512
        NUM_HEADS = 32
        HEAD_DIM = HIDDEN // NUM_HEADS

        def _fp8_roundtrip(x):
            return x.astype(jnp.float8_e4m3fn).astype(jnp.float32)
        B, S, E = hidden_states.shape
        H, D = (NUM_HEADS, HEAD_DIM)
        q = (hidden_states @ wq.T + bq).reshape(B, S, H, D)
        k = (hidden_states @ wk.T + bk).reshape(B, S, H, D)
        v = (hidden_states @ wv.T + bv).reshape(B, S, H, D)
        latent = hidden_states @ wl.T + bl
        scores = jnp.einsum('bshd,bstd->bsht', q, k) / np.sqrt(D).astype(np.float32)
        probs = jax.nn.softmax(scores, axis=-1)
        context = jnp.einsum('bsht,bstd->bshd', probs, v).reshape(B, S, E)
        return context

    def _L0_ffn_ref(x, w1, w2, w3):
        import jax, jax.numpy as jnp
        import numpy as np
        NF4_CODE = jnp.array([-1.0, -0.6961928009986877, -0.5250730514526367, -0.39491748809814453, -0.28444138169288635, -0.18477343022823334, -0.09105003625154495, 0.0, 0.07958029955625534, 0.16093020141124725, 0.24611230194568634, 0.33791524171829224, 0.44070982933044434, 0.5626170039176941, 0.7229568362236023, 1.0], dtype=jnp.float32)
        BLOCKSIZE = 64

        def nf4_quant_dequant(w):
            shape = w.shape
            flat = w.reshape(-1, BLOCKSIZE)
            absmax = jnp.max(jnp.abs(flat), axis=1, keepdims=True)
            normalized = flat / jnp.where(absmax == 0, 1.0, absmax)
            bounds = (NF4_CODE[:-1] + NF4_CODE[1:]) * 0.5
            idx = jnp.searchsorted(bounds, normalized)
            return (NF4_CODE[idx] * absmax).reshape(shape)
        dq1 = nf4_quant_dequant(w1)
        dq2 = nf4_quant_dequant(w2)
        dq3 = nf4_quant_dequant(w3)
        gate = jnp.einsum('bsd,hd->bsh', x, dq1)
        up = jnp.einsum('bsd,hd->bsh', x, dq2)
        h = jax.nn.silu(gate) * up
        return jnp.einsum('bsh,dh->bsd', h, dq3)
    x = L0_attn_hidden_states
    x = _layernorm(x + _L0_attn_ref(x, L0_attn_wq, L0_attn_bq, L0_attn_wk, L0_attn_bk, L0_attn_wv, L0_attn_bv, L0_attn_wl, L0_attn_bl), axis=-1)
    x = _layernorm(x + _L0_ffn_ref(x, L0_ffn_w1, L0_ffn_w2, L0_ffn_w3), axis=-1)
    return x

_drawn_inputs = setup_inputs


def setup_inputs(seed=0):
    import zlib

    import numpy as np

    out = dict(_drawn_inputs(seed))
    spreads = {}
    factors = {'L0_attn_wq': 3.195,
     'L0_attn_bq': 8.0,
     'L0_attn_wk': 2.993,
     'L0_attn_bk': 8.0,
     'L0_attn_bv': 8.0}
    for name, (base, spread) in spreads.items():
        noise = np.random.default_rng([zlib.crc32(name.encode()), seed]).standard_normal(out[name].shape)
        drawn = base * np.exp(spread * noise) if base else spread * noise
        out[name] = jnp.asarray(drawn.astype(out[name].dtype))
    for name, factor in factors.items():
        out[name] = (out[name] * factor).astype(out[name].dtype)
    return out
```

```python
from contextlib import ExitStack

import numpy as np

import concourse.bass as bass
from concourse import mybir

F32 = mybir.dt.float32
F32R = mybir.dt.float32r
BF16 = mybir.dt.bfloat16
ALU = mybir.AluOpType
ACT = mybir.ActivationFunctionType
AX = mybir.AxisListType

P = 128
NF4 = np.array([-1.0, -0.6961928009986877, -0.5250730514526367, -0.39491748809814453,
                -0.28444138169288635, -0.18477343022823334, -0.09105003625154495, 0.0,
                0.07958029955625534, 0.16093020141124725, 0.24611230194568634,
                0.33791524171829224, 0.44070982933044434, 0.5626170039176941,
                0.7229568362236023, 1.0], dtype=np.float32)
BOUNDS = (NF4[:-1] + NF4[1:]) * np.float32(0.5)
LEVELS = len(BOUNDS)
QBLOCK = 64
EPS = 1e-5
TINY = 1.2e-38
STEEP = float(2.0 ** 64)


def level_bound(i):
    b = BOUNDS[i]
    return float(b if NF4[i + 1] > 0 else np.nextafter(b, np.float32(2.0), dtype=np.float32))


def layer_kernel(nc, x, wq, bq, wk, bk, wv, bv, w1, w2, w3, out):
    B, S, E = x.shape
    T = B * S
    KC = E // P
    H, D = 32, 16
    HID = w1.shape[0]
    NJ = -(-HID // P)
    HLAST = HID - (NJ - 1) * P
    TB = 256
    NB = T // TB
    NT = TB // P
    Q4 = 4
    TI = TB // Q4
    GI = 16
    NG = TI // GI
    Q_TERMS = [0, 0, 0, 1, 1, 2]
    K_TERMS = [0, 1, 2, 0, 1, 0]
    KS = D * len(Q_TERMS)
    QB = HID * E // (P * QBLOCK)
    QN = -(-QB // NB)
    QF = QN * QBLOCK
    QLAP = QN * NB - QB
    N_CONST = 4
    NY = 3

    xf = x.rearrange("b s e -> (b s) e")
    of = out.rearrange("b s e -> (b s) e")
    weights = [w1, w2, w3]

    qk_d = nc.dram_tensor("qk_parts", [2, 3, E, T], BF16, kind="Internal").ap()
    v_d = nc.dram_tensor("v_feature_major", [E, T], F32, kind="Internal").ap()
    xT_d = nc.dram_tensor("x_feature_major", [E, T], F32, kind="Internal").ap()
    ctx_d = nc.dram_tensor("context_feature_major", [E, T], F32, kind="Internal").ap()
    x1_d = nc.dram_tensor("x1_feature_major", [E, T], F32, kind="Internal").ap()
    dq_d = nc.dram_tensor("dequantised", [3, HID * E], F32, kind="Internal").ap()

    def features(t, t0, n=TB):
        return t.rearrange("(c p) t -> p c t", p=P)[:, :, bass.ds(t0, n)]

    with ExitStack() as both, ExitStack() as first:
        def sb(name, shape, dt, stack=first):
            return stack.enter_context(nc.sbuf_tensor(name, shape, dt))

        def sem(name):
            return both.enter_context(nc.semaphore(name))

        def bank(name, n):
            return both.enter_context(nc.psum_tensor(name, [P, n, 512], F32))

        ident = sb("ident", [P, P], F32, both)
        ident_r = sb("ident_r", [P, P], F32R, both)
        mean_w = sb("mean_w", [P, P], F32, both)
        ones = sb("ones", [P, P], F32, both)
        half_neg = sb("half_neg", [P, NT], F32, both)
        bound_b = sb("bound_b", [P, LEVELS], F32, both)

        w_h = sb("w_h", [P, 3, KC, E], F32R)
        w_l = sb("w_l", [P, 3, KC, E], F32R)
        bias = sb("bias", [P, 3, KC], F32)
        x_tok = sb("x_tok", [P, NT, E], F32)
        xT = sb("xT", [P, KC, TB], F32)
        x_h = sb("x_h", [P, KC, TB], F32R)
        x_l = sb("x_l", [P, KC, TB], F32R)
        qk = sb("qk", [P, 2, KC, TB], F32)
        qk_part = sb("qk_part", [P, 2, 3, KC * TB], BF16)
        vT = sb("vT", [P, KC, TB], F32)
        q_st = sb("q_st", [KS, H, TB], BF16)
        k_st = sb("k_st", [KS, H, TB], BF16)
        v_bd = sb("v_bd", [P, Q4, D, TI], F32)
        prob2 = sb("prob2", [P, 2, TI, H], F32)
        prob, probT = prob2[:, 0], prob2[:, 1]
        smax = sb("smax", [P, TI], F32)
        ssum = sb("ssum", [P, TI], F32)
        srec = sb("srec", [P, TI], F32)
        ctx = sb("ctx", [Q4 * D, H, TI], F32)
        y1 = sb("y1", [P, KC, TB], F32)
        ctxT = sb("ctxT", [P, KC, TB], F32)
        sq1 = sb("sq1", [P, KC, TB], F32)
        ve1 = sb("ve1", [P, NT], F32)
        rstd1 = sb("rstd1", [P, NT], F32)
        diag1 = sb("diag1", [P, NT, P], F32)
        nf_w = sb("nf_w", [P, 3, QF], F32)
        nf_acc = sb("nf_acc", [P, 3, QF], F32)
        nf_y = sb("nf_y", [P, NY, QF], F32)
        nf_max = sb("nf_max", [P, 3, QN], F32)
        nf_den = sb("nf_den", [P, 3, QN], F32)
        nf_rec = sb("nf_rec", [P, 3, QN], F32)
        wst = prob2[:].rearrange("p a i h -> p a (i h)").rearrange("p a (m e) -> p a m e", e=E)

        first.close()

        second = both
        f1_h = sb("f1_h", [P, 2, KC, NJ * P], F32R, second)
        f1_l = sb("f1_l", [P, 2, KC, NJ * P], F32R, second)
        f3_h = sb("f3_h", [P, NJ, E], F32R, second)
        f3_l = sb("f3_l", [P, NJ, E], F32R, second)
        NS = 6
        stg = sb("stg", [P, NS + 1, KC, P], F32, second)
        x1 = sb("x1", [P, KC, TB], F32, second)
        x1_h = sb("x1_h", [P, KC, TB], F32R, second)
        x1_l = sb("x1_l", [P, KC, TB], F32R, second)
        silu = sb("silu", [P, 2, TB], F32, second)
        hid = sb("hid", [P, 2, TB], F32, second)
        hid_h = sb("hid_h", [P, NJ, TB], F32R, second)
        hid_l = sb("hid_l", [P, NJ, TB], F32R, second)
        st6 = sb("st6", [P, 2, 6], F32, second)
        mv = sb("mv", [P, 2, 2], F32, second)
        ve2 = sb("ve2", [P, 2], F32, second)
        rstd2 = sb("rstd2", [P, 2], F32, second)
        nmr2 = sb("nmr2", [P, 2], F32, second)
        o_tok = sb("o_tok", [P, 2, E], F32, second)

        ps_t = bank("ps_t", 2)
        ps_a = bank("ps_a", 2)
        ps_s = bank("ps_s", 2)
        ps_c = bank("ps_c", 2)

        s_const = sem("s_const")
        s_identr = sem("s_identr")
        s_bias = sem("s_bias")
        s_wload = [sem(f"s_wload{i}") for i in range(3)]
        s_wtr = sem("s_wtr")
        s_wh = sem("s_wh")
        s_wl = sem("s_wl")
        s_x = sem("s_x")
        s_xtr = sem("s_xtr")
        s_xT = sem("s_xT")
        s_xh = sem("s_xh")
        s_xl = sem("s_xl")
        s_proj = sem("s_proj")
        s_evac = sem("s_evac")
        s_part_h = sem("s_part_h")
        s_part_r = sem("s_part_r")
        s_part_m = sem("s_part_m")
        s_part_l = sem("s_part_l")
        s_st_parts = sem("s_st_parts")
        s_st_v = sem("s_st_v")
        s_st_xT = sem("s_st_xT")
        s_ld_stack = sem("s_ld_stack")
        s_ld_v = sem("s_ld_v")
        s_score = sem("s_score")
        s_smax = sem("s_smax")
        s_ssub = sem("s_ssub")
        s_exp = sem("s_exp")
        s_ssum = sem("s_ssum")
        s_srec = sem("s_srec")
        s_norm = sem("s_norm")
        s_probT = sem("s_probT")
        s_pv = sem("s_pv")
        s_ctx = sem("s_ctx")
        s_st_ctx = sem("s_st_ctx")
        s_ld_ln = sem("s_ld_ln")
        s_y = sem("s_y")
        s_mean = sem("s_mean")
        s_cen = sem("s_cen")
        s_sq = sem("s_sq")
        s_var = sem("s_var")
        s_ve = sem("s_ve")
        s_rstd = sem("s_rstd")
        s_diag = sem("s_diag")
        s_spread = sem("s_spread")
        s_x1 = sem("s_x1")
        s_st_x1 = sem("s_st_x1")
        s_nld = [sem(f"s_nld{i}") for i in range(3)]
        s_nmax = sem("s_nmax")
        s_nden = sem("s_nden")
        s_nrec = sem("s_nrec")
        s_nnorm = sem("s_nnorm")
        s_ny = sem("s_ny")
        s_nacc = sem("s_nacc")
        s_ndq = sem("s_ndq")
        s_nst = [sem(f"s_nst{i}") for i in range(3)]
        s_stg = [sem(f"s_stg{i}") for i in range(NS + 1)]
        s_pad = sem("s_pad")
        s_ftr = sem("s_ftr")
        s_fh = sem("s_fh")
        s_fl = sem("s_fl")
        s_x1ld = sem("s_x1ld")
        s_x1h = sem("s_x1h")
        s_x1l = sem("s_x1l")
        s_gu = sem("s_gu")
        s_silu = sem("s_silu")
        s_hid = sem("s_hid")
        s_hh = sem("s_hh")
        s_hl = sem("s_hl")
        s_down = sem("s_down")
        s_bn = sem("s_bn")
        s_mv = sem("s_mv")
        s_ve2 = sem("s_ve2")
        s_rstd2 = sem("s_rstd2")
        s_nmr2 = sem("s_nmr2")
        s_o = sem("s_o")
        s_out = [sem(f"s_out{k}") for k in range(NT)]

        def wait(eng, s, value):
            if not (isinstance(value, int) and value <= 0):
                eng.wait_ge(s, value)

        def waits(eng, *pairs):
            for s, v in pairs:
                if not isinstance(v, int):
                    eng.compute_val(v)
            for s, v in pairs:
                wait(eng, s, v)

        def hold(eng, s, value):
            eng.wait_ge(s_const, N_CONST)
            wait(eng, s, value)

        def phase_1_over(eng):
            eng.wait_ge(s_st_x1, 16 * NB)
            for w in range(3):
                eng.wait_ge(s_nst[w], 16 * NB)

        def iterations(eng, body):
            body(0, True, False, False)
            body(1, True, True, False)
            with eng.Fori(2, NB) as n:
                body(n, True, True, True)
            body(NB, False, True, True)
            body(NB + 1, False, False, True)

        def nf_slice(n):
            return 0 if isinstance(n, int) and n == 0 else (n * QN - QLAP) * QBLOCK

        def nf_view(t, at):
            return t.rearrange("(p f) -> p f", p=P)[:, bass.ds(at, QF)]

        def gu(j):
            return (ps_a, ps_s)[(j // 2) % 2][:, j % 2]

        block = both.enter_context(nc.Block())

        prep = [(w, j) for j in range(NJ) for w in range(3)]
        prep_slot = []
        prep_count = []
        used = [0] * (NS + 1)
        turn = 0
        for w, j in prep:
            if j == NJ - 1:
                s = NS
            else:
                s = turn % NS
                turn += 1
            prep_slot.append(s)
            used[s] += 1
            prep_count.append(used[s])
        prep_prev = []
        for i, s in enumerate(prep_slot):
            before = [k for k in range(i) if prep_slot[k] == s]
            prep_prev.append(before[-1] + 1 if before else 0)

        @block.sync
        def _(sp):
            for i, w in enumerate((wq, wk, wv)):
                if i == 2:
                    sp.wait_ge(s_wtr, KC)
                sp.dma_start(wst[:, i % 2], w.rearrange("(m p) e -> p m e", p=P)).then_inc(s_wload[i], 16)
            for i, v in enumerate((bq, bk, bv)):
                sp.dma_start(bias[:, i, :], v.rearrange("(c p) -> p c", p=P), allow_slow_non_contiguous=True
                             ).then_inc(s_bias, 16)

            def body(n):
                known = isinstance(n, int)
                proj, before = not known or n < NB, not known or 1 <= n <= NB
                ln, tail = not known or 2 <= n <= NB + 1, not known or n >= 3

                def store_dequantised(m, w):
                    at = sp.snap(nf_slice(m)) if not known else nf_slice(m)
                    wait(sp, s_ndq, 3 * m + w + 1)
                    sp.dma_start(nf_view(dq_d[w], at), nf_acc[:, w]).then_inc(s_nst[w], 16)

                def token(v):
                    if not known:
                        for size in (1, 2, 4):
                            sp.compute_val(v * size)
                    return v

                if proj:
                    t0 = token(n * TB)
                    wait(sp, s_xtr, n)
                    sp.dma_start(x_tok[:], xf[bass.ds(t0, TB), :].rearrange("(k p) e -> p k e", p=P)
                                 ).then_inc(s_x, 16)
                if before:
                    store_dequantised(n - 1, 1)
                if tail:
                    m = n - 3
                    t0 = token(m * TB)
                    wait(sp, s_x1, m + 1)
                    sp.dma_start(features(x1_d, t0), y1[:]).then_inc(s_st_x1, 16)
                if before:
                    store_dequantised(n - 1, 2)
                    t0 = [token((n - 1) * TB + q * TI) for q in range(Q4)]
                    waits(sp, (s_pv, NG * (n - 1)), (s_st_v, 16 * n))
                    for q in range(Q4):
                        sp.dma_start(v_bd[32 * q:32 * q + 32, q],
                                     v_d.rearrange("(t d) s -> t d s", d=D)[:, :, bass.ds(t0[q], TI)]
                                     ).then_inc(s_ld_v, 16)
                if ln:
                    m = n - 2
                    t0 = [token(m * TB + q * TI) for q in range(Q4)]
                    wait(sp, s_ctx, NG * (m + 1))
                    for q in range(Q4):
                        sp.dma_start(ctx_d.rearrange("(h d) s -> d h s", d=D)[:, :, bass.ds(t0[q], TI)],
                                     ctx[D * q:D * q + D]).then_inc(s_st_ctx, 16)
                    waits(sp, (s_y, m), (s_st_ctx, 16 * Q4 * (m + 1)))
                    sp.dma_start(ctxT[:], features(ctx_d, t0[0])).then_inc(s_ld_ln, 16)
                    wait(sp, s_st_x1, 16 * m)
                    sp.dma_start(y1[:], features(xT_d, t0[0])).then_inc(s_ld_ln, 16)
                if proj:
                    t0 = token(n * TB)
                    wait(sp, s_xT, n + 1)
                    sp.dma_start(features(xT_d, t0), xT[:]).then_inc(s_st_xT, 16)
                    wait(sp, s_part_l, 2 * (n + 1))
                    for i in range(2):
                        for part in range(3):
                            sp.dma_start(features(qk_d[i, part], t0),
                                         qk_part[:, i, part].rearrange("p (c t) -> p c t", c=KC)
                                         ).then_inc(s_st_parts, 16)
                    wait(sp, s_evac, 6 * (n + 1))
                    sp.dma_start(features(v_d, t0), vT[:]).then_inc(s_st_v, 16)
                    waits(sp, (s_st_parts, 6 * 16 * (n + 1)), (s_score, NG * n))
                    for i, (stack, terms) in enumerate(((q_st, Q_TERMS), (k_st, K_TERMS))):
                        for r, part in enumerate(terms):
                            sp.dma_start(stack[D * r:D * r + D],
                                         qk_d[i, part].rearrange("(h d) s -> d h s", d=D)[:, :, bass.ds(t0, TB)]
                                         ).then_inc(s_ld_stack, 16)
                    store_dequantised(n, 0)

            for n in range(3):
                body(n)
            with sp.Fori(3, NB) as n:
                body(n)
            for n in range(NB, NB + 3):
                body(n)
            phase_1_over(sp)
            sp.wait_ge(s_pad, 1)

            for i, (w, j) in enumerate(prep):
                wait(sp, s_ftr, prep_prev[i])
                rows = HLAST if j == NJ - 1 else P
                src = dq_d[w]
                s = prep_slot[i]
                if w < 2:
                    view = src.rearrange("(h e) -> h e", e=E)[j * P:j * P + rows, :]
                    sp.dma_start(stg[0:rows, s].rearrange("p c k -> p (c k)"), view).then_inc(s_stg[s], 16)
                else:
                    view = src.rearrange("(c p h) -> p c h", p=P, h=HID)[:, :, j * P:j * P + rows]
                    sp.dma_start(stg[:, s, :, 0:rows], view).then_inc(s_stg[s], 16)

            def token(v):
                return v if isinstance(v, int) else sp.snap(v)

            def ffn(n):
                t0 = token(n * TB)
                wait(sp, s_x1l, n)
                sp.dma_start(x1[:], features(x1_d, t0)).then_inc(s_x1ld, 16)
                if not (isinstance(n, int) and n == 0):
                    store(n - 1)

            def store(n):
                for k in range(NT):
                    t0 = token(n * TB + k * P)
                    wait(sp, s_o, NT * n + k + 1)
                    sp.dma_start(of[bass.ds(t0, P), :], o_tok[:, k]).then_inc(s_out[k], 16)

            ffn(0)
            with sp.Fori(1, NB) as n:
                ffn(n)
            store(NB - 1)
            for k in range(NT):
                sp.wait_ge(s_out[k], 16 * NB)

        @block.gpsimd
        def _(pool):
            pool.memset(ident[:], 0.0).then_inc(s_const, 1)
            pool.memset(mean_w[:], 1.0 / E).then_inc(s_const, 1)
            pool.memset(half_neg[:], -0.5).then_inc(s_const, 1)
            pool.memset(ones[:], 1.0).then_inc(s_const, 1)
            pool.wait_ge(s_const, N_CONST)
            pool.affine_select(out=ident[:], in_=ident[:], compare_op=ALU.not_equal, fill=1.0, base=0,
                               pattern=[[-1, P]], channel_multiplier=1).then_inc(s_const, 1)
            pool.memset(v_bd[:], 0.0).then_inc(s_const, 1)
            for i in range(LEVELS):
                pool.memset(bound_b[:, i:i + 1], -level_bound(i) * STEEP).then_inc(s_const, 1)

            def body(n, proj, att, ln):
                if proj:
                    for w in range(3):
                        pool.wait_ge(s_nrec, 3 * n + w + 1)
                        pool.wait_ge(s_nld[w], 16 * (n + 1))
                        v = nf_w[:, w].rearrange("p (b k) -> p b k", k=QBLOCK)
                        pool.tensor_tensor(v, v, nf_rec[:, w].unsqueeze(2).to_broadcast([P, QN, QBLOCK]),
                                           ALU.mult).then_inc(s_nnorm, 1)

                def dequantise(w):
                    pool.wait_ge(s_nacc, 3 * LEVELS * n + LEVELS * (w + 1))
                    v = nf_acc[:, w].rearrange("p (b k) -> p b k", k=QBLOCK)
                    pool.tensor_tensor(v, v, nf_max[:, w].unsqueeze(2).to_broadcast([P, QN, QBLOCK]),
                                       ALU.mult).then_inc(s_ndq, 1)

                if proj:
                    dequantise(0)
                    dequantise(1)
                if ln:
                    pool.wait_ge(s_ve, n - 1)
                    pool.tensor_tensor(rstd1[:], ve1[:], half_neg[:], ALU.pow).then_inc(s_rstd, 1)
                if proj:
                    dequantise(2)

            iterations(pool, body)

            def ffn(n):
                for k in range(NT):
                    pool.wait_ge(s_ve2, NT * n + k + 1)
                    pool.tensor_tensor(rstd2[:, k:k + 1], ve2[:, k:k + 1], half_neg[:, 0:1], ALU.pow
                                       ).then_inc(s_rstd2, 1)

            ffn(0)
            with pool.Fori(1, NB) as n:
                ffn(n)

        @block.scalar
        def _(act):
            act.wait_ge(s_const, N_CONST + 2 + LEVELS)
            act.activation(ident_r[:], ident[:], ACT.Copy).then_inc(s_identr, 1)
            for i in range(3 * KC):
                act.wait_ge(s_wtr, i + 1)
                act.activation(w_h[:, i // KC, i % KC], ps_s[:, i % 2], ACT.Copy).then_inc(s_wh, 1)
            act.wait_ge(s_bias, 48)

            def body(n, proj, att, ln):
                level = [0]

                def steep(k):
                    for _ in range(k):
                        w, i = divmod(level[0], LEVELS)
                        if i == 0:
                            act.wait_ge(s_nnorm, 3 * n + w + 1)
                        at = 3 * LEVELS * n + level[0]
                        wait(act, s_nacc, at - NY + 1)
                        act.activation(nf_y[:, level[0] % NY], nf_w[:, w], ACT.Identity,
                                       bias=bound_b[:, i:i + 1], scale=STEEP).then_inc(s_ny, 1)
                        level[0] += 1

                if proj:
                    at = nf_slice(n) if isinstance(n, int) else act.snap(nf_slice(n))
                    for w in range(3):
                        wait(act, s_ny, 3 * LEVELS * (n - 1) + LEVELS * (w + 1))
                        act.dma_start(nf_w[:, w], nf_view(weights[w].rearrange("a b -> (a b)"), at)
                                      ).then_inc(s_nld[w], 16)
                    wait(act, s_st_xT, 16 * n)
                    act.wait_ge(s_xtr, n + 1)
                    act.activation(xT[:].rearrange("p c t -> p (c t)"), ps_t[:].rearrange("p a b -> p (a b)"),
                                   ACT.Copy).then_inc(s_xT, 1)
                    act.wait_ge(s_xT, n + 1)
                    wait(act, s_proj, 6 * n)
                    act.activation(x_h[:], xT[:], ACT.Copy).then_inc(s_xh, 1)
                    for u in range(6):
                        i, half = divmod(u, 2)
                        act.wait_ge(s_proj, 6 * n + u + 1)
                        if u == 0:
                            wait(act, s_part_l, 2 * n)
                        if u == 4:
                            wait(act, s_st_v, 16 * n)
                        for a in range(2):
                            c = 2 * half + a
                            dst = qk[:, i, c] if i < 2 else vT[:, c]
                            e = act.activation(dst, ps_a[:, u % 2, a * TB:a * TB + TB], ACT.Identity,
                                               bias=bias[:, i, c:c + 1])
                        e.then_inc(s_evac, 1)
                        steep(2)
                    for i in range(2):
                        act.wait_ge(s_evac, 6 * n + 2 * i + 2)
                        if i == 0:
                            wait(act, s_st_parts, 6 * 16 * n)
                        act.activation(qk_part[:, i, 0], qk[:, i].rearrange("p c t -> p (c t)"), ACT.Copy
                                       ).then_inc(s_part_h, 1)
                    steep(LEVELS - 12)
                    for i in range(2):
                        act.wait_ge(s_part_r, 2 * n + i + 1)
                        act.activation(qk_part[:, i, 1], qk[:, i].rearrange("p c t -> p (c t)"), ACT.Copy
                                       ).then_inc(s_part_m, 1)
                if att:
                    b = n - 1
                    for g in range(NG):
                        act.wait_ge(s_ssub, NG * b + g + 1)
                        act.activation(prob[:, g * GI:(g + 1) * GI], prob[:, g * GI:(g + 1) * GI], ACT.Exp,
                                       scale=1.0 / float(np.sqrt(np.float32(D)))).then_inc(s_exp, 1)
                if ln:
                    act.wait_ge(s_cen, n - 1)
                    act.activation(sq1[:], y1[:], ACT.Square).then_inc(s_sq, 1)
                for g in range(NG):
                    if att:
                        b = n - 1
                        act.wait_ge(s_pv, NG * b + g + 1)
                        if g == 0:
                            wait(act, s_st_ctx, 16 * Q4 * b)
                        act.activation(ctx[:, :, g * GI:(g + 1) * GI],
                                       ps_c[0:Q4 * D, g % 2].rearrange("p (i h) -> p h i", h=H),
                                       ACT.Copy).then_inc(s_ctx, 1)
                    if proj:
                        steep(4)
                if proj:
                    steep(3 * LEVELS - level[0])

            iterations(act, body)
            phase_1_over(act)

            for i, (w, j) in enumerate(prep):
                act.wait_ge(s_ftr, i + 1)
                src = ps_s[:, i % 2] if i % 4 < 2 else ps_a[:, i % 2]
                if w < 2:
                    dst, src = f1_h[:, w, :, j * P:(j + 1) * P], src.rearrange("p (c k) -> p c k", c=KC)
                else:
                    dst = f3_h[:, j]
                act.activation(dst, src, ACT.Copy).then_inc(s_fh, 1)

            def ffn(n):
                act.wait_ge(s_x1ld, 16 * (n + 1))
                wait(act, s_gu, NJ * n)
                act.activation(x1_h[:], x1[:], ACT.Copy).then_inc(s_x1h, 1)

                def high(j):
                    act.wait_ge(s_hid, NJ * n + j + 1)
                    act.activation(hid_h[:, j], hid[:, j % 2], ACT.Copy).then_inc(s_hh, 1)

                for j in range(NJ):
                    at = NJ * n + j
                    act.wait_ge(s_gu, at + 1)
                    wait(act, s_hid, at - 1)
                    act.activation(silu[:, j % 2], gu(j)[:, 0:TB], ACT.Silu).then_inc(s_silu, 1)
                    if j:
                        high(j - 1)
                high(NJ - 1)
                for k in range(NT):
                    act.wait_ge(s_nmr2, NT * n + k + 1)
                    wait(act, s_out[k], 16 * n)
                    act.activation(o_tok[:, k], ps_c[:, k], ACT.Identity,
                                   bias=nmr2[:, k:k + 1], scale=rstd2[:, k:k + 1]).then_inc(s_o, 1)

            ffn(0)
            with act.Fori(1, NB) as n:
                ffn(n)

        @block.tensor
        def _(pe):
            pe.wait_ge(s_const, N_CONST + 2)
            for i in range(3):
                pe.wait_ge(s_wload[i], 16)
                for c in range(KC):
                    wait(pe, s_wl, i * KC + c - 1)
                    for m in range(KC):
                        t = pe.transpose(ps_s[:, (i * KC + c) % 2, m * P:(m + 1) * P],
                                         wst[:, i % 2, m, c * P:(c + 1) * P], ident[:])
                    t.then_inc(s_wtr, 1)
            pe.wait_ge(s_wl, 3 * KC)
            pe.wait_ge(s_wh, 3 * KC)

            def three(dst, wh, wl, rh, rl, start, stop, skip=False):
                pe.matmul(dst, wh, rh, start=start, stop=False, skip_group_check=skip)
                pe.matmul(dst, wh, rl, start=False, stop=False, skip_group_check=skip)
                return pe.matmul(dst, wl, rh, start=False, stop=stop, skip_group_check=skip)

            def body(n, proj, att, ln):
                if proj:
                    pe.wait_ge(s_x, 16 * (n + 1))
                    wait(pe, s_x1, n - 2)
                    wait(pe, s_xT, n)
                    for c in range(KC):
                        for k in range(NT):
                            t = pe.transpose(ps_t[:].rearrange("p a b -> p (a b)")[:, c * TB + k * P:c * TB + k * P + P],
                                             x_tok[:, k, c * P:(c + 1) * P], ident[:])
                    t.then_inc(s_xtr, 1)
                    pe.wait_ge(s_xh, n + 1)
                    pe.wait_ge(s_xl, n + 1)
                    for u in range(6):
                        i, half = divmod(u, 2)
                        wait(pe, s_evac, 6 * n + u - 1)
                        for a in range(2):
                            m = 2 * half + a
                            for c in range(KC):
                                t = three(ps_a[:, u % 2, a * TB:a * TB + TB],
                                          w_h[:, i, c, m * P:(m + 1) * P], w_l[:, i, c, m * P:(m + 1) * P],
                                          x_h[:, c], x_l[:, c], c == 0, c == KC - 1)
                        t.then_inc(s_proj, 1)
                if att:
                    b = n - 1
                    pe.wait_ge(s_ld_stack, 16 * 12 * (b + 1))
                    for g in range(NG):
                        wait(pe, s_ssub, NG * b + g - 1)
                        for i in range(GI):
                            for q in range(Q4):
                                s = q * TI + g * GI + i
                                t = pe.matmul(ps_s[32 * q:32 * q + 32, g % 2, i * H:(i + 1) * H],
                                              q_st[:, :, s], k_st[:, :, s], start=True, stop=True)
                        t.then_inc(s_score, 1)
                if ln:
                    pe.wait_ge(s_y, n - 1)
                    if proj:
                        pe.wait_ge(s_xT, n + 1)
                    for c in range(KC):
                        t = pe.matmul(ps_t[:, 0, 0:TB], mean_w[:], y1[:, c], start=(c == 0), stop=(c == KC - 1))
                    t.then_inc(s_mean, 1)
                if att:
                    b = n - 1
                    pe.wait_ge(s_ld_v, 16 * Q4 * (b + 1))
                    for g in range(NG):
                        pe.wait_ge(s_probT, NG * b + g + 1)
                        wait(pe, s_ctx, NG * b + g - 1)
                        for i in range(GI):
                            at = g * GI + i
                            t = pe.matmul(ps_c[0:Q4 * D, g % 2, i * H:(i + 1) * H],
                                          v_bd[:].rearrange("p a d i -> p (a d) i")[:, :, at],
                                          probT[:, at], start=True, stop=True)
                        t.then_inc(s_pv, 1)
                if ln:
                    pe.wait_ge(s_sq, n - 1)
                    for k in range(NT):
                        for c in range(KC):
                            t = pe.matmul(ps_t[:, 1, k:k + 1], sq1[:, c, k * P:(k + 1) * P], mean_w[:, 0:1],
                                          start=(c == 0), stop=(c == KC - 1))
                    t.then_inc(s_var, 1)
                    pe.wait_ge(s_diag, n - 1)
                    for k in range(NT):
                        t = pe.matmul(ps_t[:, 0, k * P:(k + 1) * P], ones[:], diag1[:, k], start=True, stop=True)
                    t.then_inc(s_spread, 1)

            iterations(pe, body)
            phase_1_over(pe)

            for i, (w, j) in enumerate(prep):
                pe.wait_ge(s_stg[prep_slot[i]], 16 * prep_count[i])
                wait(pe, s_fl, i - 3)
                dst = ps_s[:, i % 2] if i % 4 < 2 else ps_a[:, i % 2]
                for c in range(KC):
                    t = pe.transpose(dst[:, c * P:(c + 1) * P], stg[:, prep_slot[i], c], ident[:])
                t.then_inc(s_ftr, 1)
            pe.wait_ge(s_fh, len(prep))
            pe.wait_ge(s_fl, len(prep))
            pe.wait_ge(s_identr, 1)

            def ffn(n):
                pe.wait_ge(s_x1h, n + 1)
                pe.wait_ge(s_x1l, n + 1)
                for j in range(NJ):
                    at = NJ * n + j
                    wait(pe, s_hid, at - 3 if j > 3 else NJ * n)
                    for w in range(2):
                        for c in range(KC):
                            t = three(gu(j)[:, w * TB:(w + 1) * TB],
                                      f1_h[:, w, c, j * P:(j + 1) * P], f1_l[:, w, c, j * P:(j + 1) * P],
                                      x1_h[:, c], x1_l[:, c], c == 0, c == KC - 1)
                    t.then_inc(s_gu, 1)
                    if j == NJ // 2:
                        for k in range(NT):
                            wait(pe, s_o, NT * (n - 1) + k + 1)
                            for c in range(KC):
                                for part in (x1_h, x1_l):
                                    pe.matmul(ps_c[:, k, c * P:(c + 1) * P], part[:, c, k * P:(k + 1) * P],
                                              ident_r[:], start=(c == 0 and part is x1_h), stop=False,
                                              skip_group_check=True)
                pe.wait_ge(s_hh, NJ * (n + 1))
                pe.wait_ge(s_hl, NJ * (n + 1))
                for k in range(NT):
                    tok = slice(k * P, (k + 1) * P)
                    for j in range(NJ):
                        t = three(ps_c[:, k], hid_h[:, j, tok], hid_l[:, j, tok], f3_h[:, j], f3_l[:, j],
                                  False, j == NJ - 1, skip=True)
                    t.then_inc(s_down, 1)

            ffn(0)
            with pe.Fori(1, NB) as n:
                ffn(n)

        @block.vector
        def _(dve):
            for i in range(3 * KC):
                dve.wait_ge(s_wh, i + 1)
                dve.tensor_tensor(w_l[:, i // KC, i % KC], ps_s[:, i % 2], w_h[:, i // KC, i % KC].bitcast(F32),
                                  ALU.subtract).then_inc(s_wl, 1)

            def body(n, proj, att, ln):
                def scales():
                    for w in range(3):
                        dve.wait_ge(s_nld[w], 16 * (n + 1))
                        wait(dve, s_ndq, 3 * (n - 1) + w + 1)
                        dve.tensor_reduce(nf_max[:, w], nf_w[:, w].rearrange("p (b k) -> p b k", k=QBLOCK),
                                          AX.X, ALU.max, apply_absolute_value=True).then_inc(s_nmax, 1)
                    for w in range(3):
                        dve.wait_ge(s_nmax, 3 * n + w + 1)
                        dve.tensor_scalar(nf_den[:, w], nf_max[:, w], TINY, None, ALU.max).then_inc(s_nden, 1)
                    for w in range(3):
                        dve.wait_ge(s_nden, 3 * n + w + 1)
                        dve.reciprocal(nf_rec[:, w], nf_den[:, w]).then_inc(s_nrec, 1)

                def chain(w, first=0, last=LEVELS):
                    if first == 0:
                        wait(dve, s_nst[w], 16 * n)
                    for i in range(first, last):
                        at = 3 * LEVELS * n + LEVELS * w + i
                        dve.wait_ge(s_ny, at + 1)
                        y, acc = nf_y[:, (LEVELS * w + i) % NY], nf_acc[:, w]
                        if i == 0:
                            dve.tensor_scalar(acc, y, float(NF4[1]), float(NF4[0]), ALU.min, ALU.max
                                              ).then_inc(s_nacc, 1)
                        else:
                            dve.wait_ge(s_nacc, at)
                            dve.scalar_tensor_tensor(out=acc, in0=y, scalar=float(NF4[i + 1]), in1=acc,
                                                     op0=ALU.min, op1=ALU.max).then_inc(s_nacc, 1)

                if proj:
                    dve.wait_ge(s_xh, n + 1)
                    wait(dve, s_proj, 6 * n)
                    dve.tensor_tensor(x_l[:], xT[:], x_h[:].bitcast(F32), ALU.subtract).then_inc(s_xl, 1)
                    scales()
                    chain(0)
                    for i in range(2):
                        dve.wait_ge(s_part_h, 2 * n + i + 1)
                        v = qk[:, i].rearrange("p c t -> p (c t)")
                        dve.tensor_tensor(v, v, qk_part[:, i, 0], ALU.subtract).then_inc(s_part_r, 1)
                    for i in range(2):
                        dve.wait_ge(s_part_m, 2 * n + i + 1)
                        dve.tensor_tensor(qk_part[:, i, 2], qk[:, i].rearrange("p c t -> p (c t)"),
                                          qk_part[:, i, 1], ALU.subtract).then_inc(s_part_l, 1)
                if ln:
                    m = n - 2
                    dve.wait_ge(s_ld_ln, 32 * (m + 1))
                    dve.tensor_tensor(y1[:], y1[:], ctxT[:], ALU.add).then_inc(s_y, 1)
                if att:
                    b = n - 1

                    def part(t, g):
                        return t[:, g * GI:(g + 1) * GI]

                    def wide(t, g):
                        return part(t, g).unsqueeze(2).to_broadcast([P, GI, H])

                    def shift(g):
                        dve.wait_ge(s_score, NG * b + g + 1)
                        s = ps_s[:, g % 2].rearrange("p (i t) -> p i t", t=H)
                        dve.tensor_reduce(part(smax, g), s, AX.X, ALU.max).then_inc(s_smax, 1)
                        dve.wait_ge(s_smax, NG * b + g + 1)
                        dve.tensor_tensor(part(prob, g), s, wide(smax, g), ALU.subtract).then_inc(s_ssub, 1)

                    def normalise(g):
                        dve.wait_ge(s_exp, NG * b + g + 1)
                        dve.tensor_reduce(part(ssum, g), part(prob, g), AX.X, ALU.add).then_inc(s_ssum, 1)
                        dve.wait_ge(s_ssum, NG * b + g + 1)
                        dve.reciprocal(part(srec, g), part(ssum, g)).then_inc(s_srec, 1)
                        dve.wait_ge(s_srec, NG * b + g + 1)
                        dve.tensor_tensor(part(prob, g), part(prob, g), wide(srec, g), ALU.mult).then_inc(s_norm, 1)
                        dve.wait_ge(s_norm, NG * b + g + 1)
                        if g == 0:
                            wait(dve, s_pv, NG * b)
                        dve.transpose(part(probT, g).rearrange("p i h -> p (i h)"),
                                      part(prob, g).rearrange("p i h -> p (i h)")).then_inc(s_probT, 1)

                    shift(0)
                    shift(1)
                    for g in range(NG):
                        normalise(g)
                        if g + 2 < NG:
                            shift(g + 2)
                if ln:
                    dve.wait_ge(s_mean, n - 1)
                    dve.tensor_tensor(y1[:], y1[:], ps_t[:, 0, 0:TB].unsqueeze(1).to_broadcast([P, KC, TB]),
                                      ALU.subtract).then_inc(s_cen, 1)
                if proj:
                    chain(1)
                if ln:
                    dve.wait_ge(s_var, n - 1)
                    dve.tensor_scalar(ve1[:], ps_t[:, 1, 0:NT], EPS, None, ALU.add).then_inc(s_ve, 1)
                if proj:
                    chain(2, 0, 4)
                if ln:
                    dve.wait_ge(s_rstd, n - 1)
                    for k in range(NT):
                        t = dve.tensor_scalar(diag1[:, k], ident[:], rstd1[:, k:k + 1], None, ALU.mult)
                    t.then_inc(s_diag, 1)
                if proj:
                    chain(2, 4, 6)
                if ln:
                    dve.wait_ge(s_spread, n - 1)
                    dve.tensor_tensor(y1[:], y1[:], ps_t[:, 0, 0:TB].unsqueeze(1).to_broadcast([P, KC, TB]),
                                      ALU.mult).then_inc(s_x1, 1)
                if proj:
                    chain(2, 6)

            iterations(dve, body)
            phase_1_over(dve)
            dve.memset(stg[:, NS], 0.0).then_inc(s_pad, 1)

            for i, (w, j) in enumerate(prep):
                dve.wait_ge(s_fh, i + 1)
                src = ps_s[:, i % 2] if i % 4 < 2 else ps_a[:, i % 2]
                if w < 2:
                    at = (slice(None), w, slice(None), slice(j * P, (j + 1) * P))
                    hi, lo = f1_h[at], f1_l[at]
                    src = src.rearrange("p (c k) -> p c k", c=KC)
                else:
                    hi, lo = f3_h[:, j], f3_l[:, j]
                dve.tensor_tensor(lo, src, hi.bitcast(F32), ALU.subtract).then_inc(s_fl, 1)

            def ffn(n):
                dve.wait_ge(s_x1h, n + 1)
                wait(dve, s_gu, NJ * n)
                dve.tensor_tensor(x1_l[:], x1[:], x1_h[:].bitcast(F32), ALU.subtract).then_inc(s_x1l, 1)

                def low(j):
                    dve.wait_ge(s_hh, NJ * n + j + 1)
                    dve.tensor_tensor(hid_l[:, j], hid[:, j % 2], hid_h[:, j].bitcast(F32), ALU.subtract
                                      ).then_inc(s_hl, 1)

                for j in range(NJ):
                    at = NJ * n + j
                    dve.wait_ge(s_silu, at + 1)
                    wait(dve, s_hl, at - 1)
                    dve.tensor_tensor(hid[:, j % 2], silu[:, j % 2], gu(j)[:, TB:2 * TB], ALU.mult
                                      ).then_inc(s_hid, 1)
                    if j:
                        low(j - 1)
                low(NJ - 1)
                for k in range(NT):
                    at = NT * n + k + 1
                    dve.wait_ge(s_down, at)
                    dve.bn_stats(st6[:, k], ps_c[:, k]).then_inc(s_bn, 1)
                    hold(dve, s_bn, at)
                    dve.bn_aggr(mv[:, k], st6[:, k]).then_inc(s_mv, 1)
                    dve.wait_ge(s_mv, at)
                    dve.tensor_scalar(ve2[:, k:k + 1], mv[:, k, 1:2], EPS, None, ALU.add).then_inc(s_ve2, 1)
                    dve.wait_ge(s_rstd2, at)
                    wait(dve, s_o, at - NT)
                    dve.scalar_tensor_tensor(out=nmr2[:, k:k + 1], in0=mv[:, k, 0:1], scalar=-1.0,
                                             in1=rstd2[:, k:k + 1], op0=ALU.mult, op1=ALU.mult
                                             ).then_inc(s_nmr2, 1)

            ffn(0)
            with dve.Fori(1, NB) as n:
                ffn(n)


_INS = ["L0_attn_hidden_states", "L0_attn_wq", "L0_attn_bq", "L0_attn_wk", "L0_attn_bk", "L0_attn_wv",
        "L0_attn_bv", "L0_ffn_w1", "L0_ffn_w2", "L0_ffn_w3"]


def kernel(**inputs):
    import concourse.bacc as _bacc
    from concourse.bass_utils import run_bass_kernel_spmd as _run

    nc = _bacc.Bacc("TRN2", target_bir_lowering=False, num_devices=1)
    arrays, args = {}, []
    for name in _INS:
        a = np.ascontiguousarray(inputs[name])
        arrays[f"in_{name}"] = a
        args.append(nc.dram_tensor(f"in_{name}", a.shape, mybir.dt.from_np(a.dtype), kind="ExternalInput").ap())
    shape = inputs["L0_attn_hidden_states"].shape
    args.append(nc.dram_tensor("out_0", shape, F32, kind="ExternalOutput").ap())
    layer_kernel(nc, *args)
    r = _run(nc, [arrays], core_ids=[0])
    return r.results[0]["out_0"]
```

```python
from contextlib import ExitStack

import numpy as np

import concourse.bass as bass
from concourse import mybir

F32 = mybir.dt.float32
F32R = mybir.dt.float32r
BF16 = mybir.dt.bfloat16
ALU = mybir.AluOpType
ACT = mybir.ActivationFunctionType
AX = mybir.AxisListType

P = 128
NF4 = np.array([-1.0, -0.6961928009986877, -0.5250730514526367, -0.39491748809814453,
                -0.28444138169288635, -0.18477343022823334, -0.09105003625154495, 0.0,
                0.07958029955625534, 0.16093020141124725, 0.24611230194568634,
                0.33791524171829224, 0.44070982933044434, 0.5626170039176941,
                0.7229568362236023, 1.0], dtype=np.float32)
BOUNDS = (NF4[:-1] + NF4[1:]) * np.float32(0.5)
LEVELS = len(BOUNDS)
QBLOCK = 64
EPS = 1e-5
TINY = 1.2e-38
STEEP = float(2.0 ** 64)


def level_bound(i):
    b = BOUNDS[i]
    return float(b if NF4[i + 1] > 0 else np.nextafter(b, np.float32(2.0), dtype=np.float32))


def layer_kernel(nc, x, wq, bq, wk, bk, wv, bv, w1, w2, w3, out):
    B, S, E = x.shape
    T = B * S
    KC = E // P
    H, D = 32, 16
    HID = w1.shape[0]
    NJ = -(-HID // P)
    HLAST = HID - (NJ - 1) * P
    TB = 256
    NB = T // TB
    NT = TB // P
    Q4 = 4
    TI = TB // Q4
    GI = 16
    NG = TI // GI
    Q_TERMS = [0, 0, 0, 1, 1, 2]
    K_TERMS = [0, 1, 2, 0, 1, 0]
    KS = D * len(Q_TERMS)
    JA = 6
    J_OF = [range(JA), range(JA, NJ)]
    BLOCKS_A = JA * P * E // (P * QBLOCK)
    BLOCKS_B = (HID - JA * P) * E // (P * QBLOCK)
    BLOCKS_3 = HID * E // (P * QBLOCK)
    NA, N_B, N3 = (-(-b // NB) for b in (BLOCKS_A, BLOCKS_B, BLOCKS_3))
    QN = 2 * NA + N3
    FA, FB, F3 = NA * QBLOCK, N_B * QBLOCK, N3 * QBLOCK
    CHAINS = [(0, 2 * FA), (2 * FA, 2 * FA + F3)]
    FY = max(2 * FA, F3, 2 * FB)
    STEPS = 2 * LEVELS
    LATE = 4
    N_CONST = 4
    NY, NYB = 5, 3

    xf = x.rearrange("b s e -> (b s) e")
    of = out.rearrange("b s e -> (b s) e")
    flat = [w.rearrange("a b -> (a b)") for w in (w1, w2, w3)]

    qk_d = nc.dram_tensor("qk_parts", [2, 3, E, T], BF16, kind="Internal").ap()
    v_d = nc.dram_tensor("v_feature_major", [E, T], F32, kind="Internal").ap()
    xT_d = nc.dram_tensor("x_feature_major", [E, T], F32, kind="Internal").ap()
    ctx_d = nc.dram_tensor("context_feature_major", [E, T], F32, kind="Internal").ap()
    x1_d = nc.dram_tensor("x1_feature_major", [E, T], F32, kind="Internal").ap()
    dq_d = nc.dram_tensor("dequantised", [3, HID * E], F32, kind="Internal").ap()

    def features(t, t0, n=TB):
        return t.rearrange("(c p) t -> p c t", p=P)[:, :, bass.ds(t0, n)]

    with ExitStack() as both, ExitStack() as first:
        def sb(name, shape, dt, stack=first):
            return stack.enter_context(nc.sbuf_tensor(name, shape, dt))

        def sem(name):
            return both.enter_context(nc.semaphore(name))

        def bank(name, n):
            return both.enter_context(nc.psum_tensor(name, [P, n, 512], F32))

        ident = sb("ident", [P, P], F32, both)
        ident_r = sb("ident_r", [P, P], F32R, both)
        mean_w = sb("mean_w", [P, P], F32, both)
        ones = sb("ones", [P, P], F32, both)
        half_neg = sb("half_neg", [P, NT], F32, both)
        bound_b = sb("bound_b", [P, LEVELS], F32, both)

        w_h = sb("w_h", [P, 3, KC, E], F32R)
        w_l = sb("w_l", [P, 3, KC, E], F32R)
        bias = sb("bias", [P, 3, KC], F32)
        x_tok = sb("x_tok", [P, NT, E], F32)
        xT = sb("xT", [P, KC, TB], F32)
        x_h = sb("x_h", [P, KC, TB], F32R)
        x_l = sb("x_l", [P, KC, TB], F32R)
        qk = sb("qk", [P, 2, KC, TB], F32)
        qk_part = sb("qk_part", [P, 2, 3, KC * TB], BF16)
        vT = sb("vT", [P, KC, TB], F32)
        q_st = sb("q_st", [KS, H, TB], BF16)
        k_st = sb("k_st", [KS, H, TB], BF16)
        v_bd = sb("v_bd", [P, Q4, D, TI], F32)
        prob2 = sb("prob2", [P, 2, TI, H], F32)
        prob, probT = prob2[:, 0], prob2[:, 1]
        smax = sb("smax", [P, TI], F32)
        ssum = sb("ssum", [P, TI], F32)
        srec = sb("srec", [P, TI], F32)
        ctx = sb("ctx", [Q4 * D, H, TI], F32)
        y1 = sb("y1", [P, KC, TB], F32)
        ctxT = sb("ctxT", [P, KC, TB], F32)
        sq1 = ctxT
        ve1 = sb("ve1", [P, NT], F32)
        rstd1 = sb("rstd1", [P, NT], F32)
        diag1 = sb("diag1", [P, NT, P], F32)
        nf_raw = sb("nf_raw", [P, QN * QBLOCK], F32)
        nf_w = sb("nf_w", [P, QN * QBLOCK], F32)
        nf_acc = sb("nf_acc", [P, QN * QBLOCK], F32)
        nf_y = sb("nf_y", [P, NY, FY], F32)
        nf_max = sb("nf_max", [P, QN], F32)
        nf_den = sb("nf_den", [P, QN], F32)
        nf_rec = sb("nf_rec", [P, QN], F32)
        nf_scale = sb("nf_scale", [P, QN], F32)
        wst = prob2[:].rearrange("p a i h -> p a (i h)").rearrange("p a (m e) -> p a m e", e=E)

        first.close()

        second = both
        f1_h = sb("f1_h", [P, 2, KC, NJ * P], F32R, second)
        f1_l = sb("f1_l", [P, 2, KC, NJ * P], F32R, second)
        f3_h = sb("f3_h", [P, NJ, E], F32R, second)
        f3_l = sb("f3_l", [P, NJ, E], F32R, second)
        NS = 4
        stg = sb("stg", [P, NS + 1, KC, P], F32, second)
        x1 = sb("x1", [P, KC, TB], F32, second)
        x1_h = sb("x1_h", [P, KC, TB], F32R, second)
        x1_l = sb("x1_l", [P, KC, TB], F32R, second)
        silu = sb("silu", [P, 2, TB], F32, second)
        hid = silu
        hid_h = sb("hid_h", [P, JA, TB], F32R, second)
        hid_l = sb("hid_l", [P, JA, TB], F32R, second)
        part = sb("part", [P, T // P, E], F32, second)
        nb_w = sb("nb_w", [P, 2 * FB], F32, second)
        nb_acc = sb("nb_acc", [P, 2 * FB], F32, second)
        rest = stg[:, 0:NS].rearrange("p s c k -> p (s c k)")
        nb_y = rest[:, 0:NYB * 2 * FB].rearrange("p (y f) -> p y f", y=NYB)
        o_tok = rest[:, 0:NT * E].rearrange("p (k e) -> p k e", k=NT)
        nb_max = sb("nb_max", [P, 2 * N_B], F32, second)
        nb_den = sb("nb_den", [P, 2 * N_B], F32, second)
        nb_rec = sb("nb_rec", [P, 2 * N_B], F32, second)
        st6 = sb("st6", [P, 2, 6], F32, second)
        mv = sb("mv", [P, 2, 2], F32, second)
        ve2 = sb("ve2", [P, 2], F32, second)
        rstd2 = sb("rstd2", [P, 2], F32, second)
        nmr2 = sb("nmr2", [P, 2], F32, second)

        ps_t = bank("ps_t", 2)
        ps_a = bank("ps_a", 2)
        ps_s = bank("ps_s", 2)
        ps_c = bank("ps_c", 2)

        s_const = sem("s_const")
        s_identr = sem("s_identr")
        s_bias = sem("s_bias")
        s_wload = [sem(f"s_wload{i}") for i in range(3)]
        s_wtr = sem("s_wtr")
        s_wh = sem("s_wh")
        s_wl = sem("s_wl")
        s_x = sem("s_x")
        s_xtr = sem("s_xtr")
        s_xT = sem("s_xT")
        s_xh = sem("s_xh")
        s_xl = sem("s_xl")
        s_proj = sem("s_proj")
        s_evac = sem("s_evac")
        s_part_h = sem("s_part_h")
        s_part_r = sem("s_part_r")
        s_part_m = sem("s_part_m")
        s_part_l = sem("s_part_l")
        s_st_q = sem("s_st_q")
        s_st_k = sem("s_st_k")
        s_st_v = sem("s_st_v")
        s_st_xT = sem("s_st_xT")
        s_ld_stack = sem("s_ld_stack")
        s_ld_v = sem("s_ld_v")
        s_score = sem("s_score")
        s_smax = sem("s_smax")
        s_ssub = sem("s_ssub")
        s_exp = sem("s_exp")
        s_ssum = sem("s_ssum")
        s_srec = sem("s_srec")
        s_norm = sem("s_norm")
        s_probT = sem("s_probT")
        s_pv = sem("s_pv")
        s_ctx = sem("s_ctx")
        s_st_ctx = sem("s_st_ctx")
        s_ld_ln = sem("s_ld_ln")
        s_y = sem("s_y")
        s_mean = sem("s_mean")
        s_cen = sem("s_cen")
        s_sq = sem("s_sq")
        s_var = sem("s_var")
        s_ve = sem("s_ve")
        s_rstd = sem("s_rstd")
        s_diag = sem("s_diag")
        s_spread = sem("s_spread")
        s_x1 = sem("s_x1")
        s_st_x1 = sem("s_st_x1")
        s_nld = sem("s_nld")
        s_nmax = sem("s_nmax")
        s_nden = sem("s_nden")
        s_nrec = sem("s_nrec")
        s_nscale = sem("s_nscale")
        s_nnorm = sem("s_nnorm")
        s_ny = sem("s_ny")
        s_nacc = sem("s_nacc")
        s_ndq = sem("s_ndq")
        s_nst = sem("s_nst")
        s_bld = sem("s_bld")
        s_bmax = sem("s_bmax")
        s_bden = sem("s_bden")
        s_brec = sem("s_brec")
        s_bnorm = sem("s_bnorm")
        s_by = sem("s_by")
        s_bacc = sem("s_bacc")
        s_bdq = sem("s_bdq")
        s_bst = sem("s_bst")
        s_stg = [sem(f"s_stg{i}") for i in range(NS + 1)]
        s_pad = sem("s_pad")
        s_ftr = sem("s_ftr")
        s_fh = sem("s_fh")
        s_fl = sem("s_fl")
        s_x1ld = sem("s_x1ld")
        s_x1h = sem("s_x1h")
        s_x1l = sem("s_x1l")
        s_gu = sem("s_gu")
        s_silu = sem("s_silu")
        s_hid = sem("s_hid")
        s_hh = sem("s_hh")
        s_hl = sem("s_hl")
        s_down = sem("s_down")
        s_part = sem("s_part")
        s_sum = sem("s_sum")
        s_bn = sem("s_bn")
        s_mv = sem("s_mv")
        s_ve2 = sem("s_ve2")
        s_rstd2 = sem("s_rstd2")
        s_nmr2 = sem("s_nmr2")
        s_o = sem("s_o")
        s_out = [sem(f"s_out{k}") for k in range(NT)]

        def wait(eng, s, value):
            if not (isinstance(value, int) and value <= 0):
                eng.wait_ge(s, value)

        def waits(eng, *pairs):
            for s, v in pairs:
                if not isinstance(v, int):
                    eng.compute_val(v)
            for s, v in pairs:
                wait(eng, s, v)

        def hold(eng, s, value):
            eng.wait_ge(s_const, N_CONST)
            wait(eng, s, value)

        def phase_1_over(eng):
            eng.wait_ge(s_st_x1, 16 * NB)
            eng.wait_ge(s_nst, 3 * 16 * NB)

        def iterations(eng, body):
            body(0, True, False, False)
            body(1, True, True, False)
            with eng.Fori(2, NB) as n:
                body(n, True, True, True)
            body(NB, False, True, True)
            body(NB + 1, False, False, True)

        def start_of(n, count, blocks):
            lap = count * NB - blocks
            return 0 if isinstance(n, int) and n == 0 else (n * count - lap) * QBLOCK

        def rows_view(t, lo, hi):
            return t[lo * E:hi * E].rearrange("(p f) -> p f", p=P)

        PARTS = [(rows_view(flat[w], 0, hi), rows_view(dq_d[w], 0, hi), blocks, count, col)
                 for w, hi, blocks, count, col in ((0, JA * P, BLOCKS_A, NA, 0), (1, JA * P, BLOCKS_A, NA, FA),
                                                   (2, HID, BLOCKS_3, N3, 2 * FA))]
        PARTS_B = [(rows_view(flat[w], JA * P, HID), rows_view(dq_d[w], JA * P, HID), w * FB) for w in range(2)]

        def blocks_of(t):
            return t.rearrange("p (b k) -> p b k", k=QBLOCK)

        def gu(j):
            return (ps_a, ps_s)[(j // 2) % 2][:, j % 2]

        block = both.enter_context(nc.Block())

        prep = [(w, j) for j in range(NJ - 1) for w in range(3)]
        PREP_OF = [range(3 * JA), range(3 * JA, 3 * NJ)]
        for w in range(3):
            prep.insert(3 * JA + 4 * (w + 1), (w, NJ - 1))
        prep_slot = []
        prep_count = []
        used = [0] * (NS + 1)
        turn = 0
        for w, j in prep:
            if j == NJ - 1:
                s = NS
            else:
                s = turn % NS
                turn += 1
            prep_slot.append(s)
            used[s] += 1
            prep_count.append(used[s])
        def prep_bank(i):
            return ps_s[:, i % 2] if i % 4 < 2 else ps_a[:, i % 2]

        prep_prev = []
        for i, s in enumerate(prep_slot):
            before = [k for k in range(i) if prep_slot[k] == s]
            prep_prev.append(before[-1] + 1 if before else 0)

        @block.sync
        def _(sp):
            for i, w in enumerate((wq, wk, wv)):
                if i == 2:
                    sp.wait_ge(s_wtr, KC)
                sp.dma_start(wst[:, i % 2], w.rearrange("(m p) e -> p m e", p=P)).then_inc(s_wload[i], 16)
            for i, v in enumerate((bq, bk, bv)):
                sp.dma_start(bias[:, i, :], v.rearrange("(c p) -> p c", p=P), allow_slow_non_contiguous=True
                             ).then_inc(s_bias, 16)

            def token(v):
                if not isinstance(v, int):
                    for size in (1, 2, 4):
                        sp.compute_val(v * size)
                return v

            def places(n):
                at = [start_of(n, count, blocks) for _, _, blocks, count, _ in PARTS]
                for v in at:
                    if not isinstance(v, int):
                        sp.compute_val(v * 4)
                return at

            def load_x(n):
                t0 = token(n * TB)
                wait(sp, s_xtr, n)
                sp.dma_start(x_tok[:], xf[bass.ds(t0, TB), :].rearrange("(k p) e -> p k e", p=P)
                             ).then_inc(s_x, 16)

            def load_slice(n):
                at = places(n)
                wait(sp, s_nnorm, 2 * n)
                for w, (src, _, _, count, col) in enumerate(PARTS):
                    sp.dma_start(nf_raw[:, col:col + count * QBLOCK],
                                 src[:, bass.ds(at[w], count * QBLOCK)]).then_inc(s_nld, 16)

            def body(n):
                known = isinstance(n, int)
                proj, before = not known or n < NB, not known or 1 <= n <= NB
                ln, tail = not known or 2 <= n <= NB + 1, not known or n >= 3

                def token(v):
                    if not known:
                        for size in (1, 2, 4):
                            sp.compute_val(v * size)
                    return v

                if tail:
                    m = n - 3
                    t0 = token(m * TB)
                    wait(sp, s_x1, m + 1)
                    sp.dma_start(features(x1_d, t0), y1[:]).then_inc(s_st_x1, 16)
                if ln:
                    m = n - 2
                    tm = [token(m * TB + q * TI) for q in range(Q4)]
                    wait(sp, s_ctx, NG * (m + 1))
                    for q in range(Q4):
                        sp.dma_start(ctx_d.rearrange("(h d) s -> d h s", d=D)[:, :, bass.ds(tm[q], TI)],
                                     ctx[D * q:D * q + D]).then_inc(s_st_ctx, 16)
                if before:
                    t0 = [token((n - 1) * TB + q * TI) for q in range(Q4)]
                    waits(sp, (s_pv, NG * (n - 1)), (s_st_v, 16 * n))
                    for q in range(Q4):
                        sp.dma_start(v_bd[32 * q:32 * q + 32, q],
                                     v_d.rearrange("(t d) s -> t d s", d=D)[:, :, bass.ds(t0[q], TI)]
                                     ).then_inc(s_ld_v, 16)
                if ln:
                    waits(sp, (s_var, m), (s_st_ctx, 16 * Q4 * (m + 1)))
                    sp.dma_start(ctxT[:], features(ctx_d, tm[0])).then_inc(s_ld_ln, 16)
                    wait(sp, s_st_x1, 16 * m)
                    sp.dma_start(y1[:], features(xT_d, tm[0])).then_inc(s_ld_ln, 16)
                if before:
                    at = places(n - 1)
                    for w, (_, dst, _, count, col) in enumerate(PARTS):
                        if w != 1:
                            wait(sp, s_ndq, 2 * (n - 1) + (1 if w == 0 else 2))
                        sp.dma_start(dst[:, bass.ds(at[w], count * QBLOCK)],
                                     nf_acc[:, col:col + count * QBLOCK]).then_inc(s_nst, 16)
                if proj:
                    t0 = token(n * TB)
                    wait(sp, s_xT, n + 1)
                    sp.dma_start(features(xT_d, t0), xT[:]).then_inc(s_st_xT, 16)
                    if not known or n + 1 < NB:
                        load_x(n + 1)
                        load_slice(n + 1)
                    t0 = token(n * TB)
                    for i, s_st in enumerate((s_st_q, s_st_k)):
                        wait(sp, s_part_l, 2 * n + i + 1)
                        for part in range(3):
                            sp.dma_start(features(qk_d[i, part], t0),
                                         qk_part[:, i, part].rearrange("p (c t) -> p c t", c=KC)
                                         ).then_inc(s_st, 16)
                    for i, (stack, terms, s_st) in enumerate(((q_st, Q_TERMS, s_st_q), (k_st, K_TERMS, s_st_k))):
                        waits(sp, (s_st, 3 * 16 * (n + 1)), (s_score, NG * n))
                        for r, part in enumerate(terms):
                            sp.dma_start(stack[D * r:D * r + D],
                                         qk_d[i, part].rearrange("(h d) s -> d h s", d=D)[:, :, bass.ds(t0, TB)]
                                         ).then_inc(s_ld_stack, 16)
                        if i == 0:
                            wait(sp, s_evac, 6 * (n + 1))
                            sp.dma_start(features(v_d, t0), vT[:]).then_inc(s_st_v, 16)

            load_x(0)
            load_slice(0)
            for n in range(3):
                body(n)
            with sp.Fori(3, NB - 1) as n:
                body(n)
            for n in range(NB - 1, NB + 3):
                body(n)
            phase_1_over(sp)
            sp.wait_ge(s_pad, 1)

            def stage(half):
                for i in PREP_OF[half]:
                    w, j = prep[i]
                    wait(sp, s_ftr, prep_prev[i])
                    rows = HLAST if j == NJ - 1 else P
                    s = prep_slot[i]
                    if w < 2:
                        view = dq_d[w].rearrange("(h e) -> h e", e=E)[j * P:j * P + rows, :]
                        sp.dma_start(stg[0:rows, s].rearrange("p c k -> p (c k)"), view).then_inc(s_stg[s], 16)
                    else:
                        view = dq_d[w].rearrange("(c p h) -> p c h", p=P, h=HID)[:, :, j * P:j * P + rows]
                        sp.dma_start(stg[:, s, :, 0:rows], view).then_inc(s_stg[s], 16)

            def known(n):
                return isinstance(n, int)

            def offset(v):
                if not known(v):
                    sp.compute_val(v * 4)
                return v

            def load_x1(half, n):
                t0 = offset(n * TB)
                wait(sp, s_x1l, NB * half + n)
                sp.dma_start(x1[:], features(x1_d, t0)).then_inc(s_x1ld, 16)

            def store_slice(n):
                at = offset(start_of(n, N_B, BLOCKS_B))
                wait(sp, s_bdq, n + 1)
                for _, dst, col in PARTS_B:
                    sp.dma_start(dst[:, bass.ds(at, FB)], nb_acc[:, col:col + FB]).then_inc(s_bst, 16)

            def store(n):
                for k in range(NT):
                    t0 = offset(n * TB + k * P)
                    wait(sp, s_o, NT * n + k + 1)
                    sp.dma_start(of[bass.ds(t0, P), :], o_tok[:, k]).then_inc(s_out[k], 16)

            stage(0)
            load_x1(0, 0)
            load_x1(0, 1)
            store_slice(0)
            with sp.Fori(2, NB) as n:
                load_x1(0, n)
                store_slice(n - 1)
            load_x1(1, 0)
            store_slice(NB - 1)
            sp.wait_ge(s_bst, 2 * 16 * NB)
            stage(1)
            load_x1(1, 1)
            store(0)
            with sp.Fori(2, NB) as n:
                load_x1(1, n)
                store(n - 1)
            store(NB - 1)
            for k in range(NT):
                sp.wait_ge(s_out[k], 16 * NB)

        @block.gpsimd
        def _(pool):
            pool.memset(ident[:], 0.0).then_inc(s_const, 1)
            pool.memset(mean_w[:], 1.0 / E).then_inc(s_const, 1)
            pool.memset(half_neg[:], -0.5).then_inc(s_const, 1)
            pool.memset(ones[:], 1.0).then_inc(s_const, 1)
            pool.wait_ge(s_const, N_CONST)
            pool.affine_select(out=ident[:], in_=ident[:], compare_op=ALU.not_equal, fill=1.0, base=0,
                               pattern=[[-1, P]], channel_multiplier=1).then_inc(s_const, 1)
            pool.memset(v_bd[:], 0.0).then_inc(s_const, 1)
            for i in range(LEVELS):
                pool.memset(bound_b[:, i:i + 1], -level_bound(i) * STEEP).then_inc(s_const, 1)

            def body(n, proj, att, ln):
                if proj:
                    pool.wait_ge(s_xh, n + 1)
                    wait(pool, s_proj, 6 * n)
                    pool.tensor_tensor(x_l[:], xT[:], x_h[:].bitcast(F32), ALU.subtract).then_inc(s_xl, 1)
                    pool.wait_ge(s_nrec, n + 1)
                    wait(pool, s_ny, STEPS * n)
                    for lo, hi in CHAINS:
                        b0, b1 = lo // QBLOCK, hi // QBLOCK
                        pool.tensor_tensor(blocks_of(nf_w[:, lo:hi]), blocks_of(nf_raw[:, lo:hi]),
                                           nf_rec[:, b0:b1].unsqueeze(2).to_broadcast([P, b1 - b0, QBLOCK]),
                                           ALU.mult).then_inc(s_nnorm, 1)
                if att:
                    for i, (lo, hi) in enumerate(CHAINS):
                        if i == 0:
                            pool.wait_ge(s_nacc, STEPS * n)
                        v = blocks_of(nf_acc[:, lo:hi])
                        b0, b1 = lo // QBLOCK, hi // QBLOCK
                        pool.tensor_tensor(v, v, nf_scale[:, b0:b1].unsqueeze(2).to_broadcast([P, b1 - b0, QBLOCK]),
                                           ALU.mult).then_inc(s_ndq, 1)
                if proj:
                    wait(pool, s_ndq, 2 * n)
                    pool.tensor_tensor(nf_scale[:], nf_max[:], ones[:, 0:QN], ALU.mult).then_inc(s_nscale, 1)

                def remainders(i):
                    v = qk[:, i].rearrange("p c t -> p (c t)")
                    pool.wait_ge(s_part_h, 2 * n + i + 1)
                    pool.tensor_tensor(v, v, qk_part[:, i, 0], ALU.subtract).then_inc(s_part_r, 1)
                    pool.wait_ge(s_part_m, 2 * n + i + 1)
                    pool.tensor_tensor(qk_part[:, i, 2], v, qk_part[:, i, 1], ALU.subtract).then_inc(s_part_l, 1)

                if proj:
                    remainders(0)
                if ln:
                    pool.wait_ge(s_ld_ln, 32 * (n - 1))
                    pool.tensor_tensor(y1[:], y1[:], ctxT[:], ALU.add).then_inc(s_y, 1)
                if proj:
                    remainders(1)
                if ln:
                    pool.wait_ge(s_ve, n - 1)
                    pool.tensor_tensor(rstd1[:], ve1[:], half_neg[:], ALU.pow).then_inc(s_rstd, 1)
                    pool.wait_ge(s_rstd, n - 1)
                    pool.tensor_tensor(diag1[:], ident[:].unsqueeze(1).to_broadcast([P, NT, P]),
                                       rstd1[:].unsqueeze(2).to_broadcast([P, NT, P]), ALU.mult
                                       ).then_inc(s_diag, 1)

            iterations(pool, body)

            phase_1_over(pool)

            def slice_b(n):
                pool.wait_ge(s_brec, n + 1)
                v = blocks_of(nb_w[:])
                pool.tensor_tensor(v, v, nb_rec[:].unsqueeze(2).to_broadcast([P, 2 * N_B, QBLOCK]), ALU.mult
                                   ).then_inc(s_bnorm, 1)
                pool.wait_ge(s_bacc, LEVELS * (n + 1))
                v = blocks_of(nb_acc[:])
                pool.tensor_tensor(v, v, nb_max[:].unsqueeze(2).to_broadcast([P, 2 * N_B, QBLOCK]), ALU.mult
                                   ).then_inc(s_bdq, 1)

            with pool.Fori(0, NB) as n:
                slice_b(n)

            with pool.Fori(0, NB) as n:
                for k in range(NT):
                    pool.wait_ge(s_ve2, NT * n + k + 1)
                    pool.tensor_tensor(rstd2[:, k:k + 1], ve2[:, k:k + 1], half_neg[:, 0:1], ALU.pow
                                       ).then_inc(s_rstd2, 1)

        @block.scalar
        def _(act):
            act.wait_ge(s_const, N_CONST + 2 + LEVELS)
            act.activation(ident_r[:], ident[:], ACT.Copy).then_inc(s_identr, 1)
            for i in range(3 * KC):
                act.wait_ge(s_wtr, i + 1)
                act.activation(w_h[:, i // KC, i % KC], ps_s[:, i % 2], ACT.Copy).then_inc(s_wh, 1)
            act.wait_ge(s_bias, 48)

            def body(n, proj, att, ln):
                def steep(lo, hi, unit):
                    for step in range(lo, hi):
                        i, c = divmod(step, 2)
                        if step < 2:
                            act.wait_ge(s_nnorm, 2 * unit + c + 1)
                        at = STEPS * unit + step
                        wait(act, s_nacc, at - NY + 1)
                        a, b = CHAINS[c]
                        act.activation(nf_y[:, step % NY, 0:b - a], nf_w[:, a:b], ACT.Identity,
                                       bias=bound_b[:, i:i + 1], scale=STEEP).then_inc(s_ny, 1)

                step = [0]

                def some(k):
                    hi = min(step[0] + k, STEPS - LATE)
                    steep(step[0], hi, n)
                    step[0] = hi

                def exp(g):
                    if att:
                        act.wait_ge(s_ssub, NG * (n - 1) + g + 1)
                        act.activation(prob[:, g * GI:(g + 1) * GI], prob[:, g * GI:(g + 1) * GI], ACT.Exp,
                                       scale=1.0 / float(np.sqrt(np.float32(D)))).then_inc(s_exp, 1)

                if proj:
                    wait(act, s_st_xT, 16 * n)
                    act.wait_ge(s_xtr, n + 1)
                    act.activation(xT[:].rearrange("p c t -> p (c t)"), ps_t[:].rearrange("p a b -> p (a b)"),
                                   ACT.Copy).then_inc(s_xT, 1)
                    act.wait_ge(s_xT, n + 1)
                    wait(act, s_proj, 6 * n)
                    act.activation(x_h[:], xT[:], ACT.Copy).then_inc(s_xh, 1)
                if att:
                    steep(STEPS - LATE, STEPS, n - 1)
                if proj:
                    some(3)
                if not proj:
                    for g in range(NG):
                        exp(g)
                if proj:
                    def middle(i):
                        act.wait_ge(s_part_r, 2 * n + i + 1)
                        act.activation(qk_part[:, i, 1], qk[:, i].rearrange("p c t -> p (c t)"), ACT.Copy
                                       ).then_inc(s_part_m, 1)

                    for u in range(6):
                        i, half = divmod(u, 2)
                        act.wait_ge(s_proj, 6 * n + u + 1)
                        if u % 2 == 0:
                            if i < 2:
                                wait(act, s_part_l, 2 * (n - 1) + i + 1)
                            else:
                                wait(act, s_st_v, 16 * n)
                        for a in range(2):
                            c = 2 * half + a
                            dst = qk[:, i, c] if i < 2 else vT[:, c]
                            e = act.activation(dst, ps_a[:, u % 2, a * TB:a * TB + TB], ACT.Identity,
                                               bias=bias[:, i, c:c + 1])
                        e.then_inc(s_evac, 1)
                        if u == 0:
                            exp(0)
                            exp(1)
                        if u in (2, 4):
                            middle(u // 2 - 1)
                        if u in (1, 3):
                            act.wait_ge(s_evac, 6 * n + u + 1)
                            wait(act, (s_st_q, s_st_k)[i], 3 * 16 * n)
                            act.activation(qk_part[:, i, 0], qk[:, i].rearrange("p c t -> p (c t)"), ACT.Copy
                                           ).then_inc(s_part_h, 1)
                        if u in (1, 2):
                            exp(u + 1)
                        if u > 1:
                            some(1)
                for g in range(NG):
                    if att:
                        b = n - 1
                        act.wait_ge(s_pv, NG * b + g + 1)
                        if g == 0:
                            wait(act, s_st_ctx, 16 * Q4 * b)
                        act.activation(ctx[:, :, g * GI:(g + 1) * GI],
                                       ps_c[0:Q4 * D, g % 2].rearrange("p (i h) -> p h i", h=H),
                                       ACT.Copy).then_inc(s_ctx, 1)
                    if g == 1 and ln:
                        act.wait_ge(s_cen, n - 1)
                        act.activation(sq1[:], y1[:], ACT.Square).then_inc(s_sq, 1)
                    if proj:
                        some(2)
                if proj:
                    some(STEPS)

            iterations(act, body)
            phase_1_over(act)

            def prepare(half):
                for i in PREP_OF[half]:
                    w, j = prep[i]
                    act.wait_ge(s_ftr, i + 1)
                    src = prep_bank(i)
                    if w < 2:
                        dst, src = f1_h[:, w, :, j * P:(j + 1) * P], src.rearrange("p (c k) -> p c k", c=KC)
                    else:
                        dst = f3_h[:, j]
                    act.activation(dst, src, ACT.Copy).then_inc(s_fh, 1)

            def load_b(n):
                at = start_of(n, N_B, BLOCKS_B)
                if not isinstance(n, int):
                    act.compute_val(at * 4)
                wait(act, s_by, LEVELS * n)
                for src, _, col in PARTS_B:
                    act.dma_start(nb_w[:, col:col + FB], src[:, bass.ds(at, FB)]).then_inc(s_bld, 16)

            def split(block_n, done):
                act.wait_ge(s_x1ld, 16 * (block_n + 1))
                wait(act, s_gu, done)
                act.activation(x1_h[:], x1[:], ACT.Copy).then_inc(s_x1h, 1)

            def ffn(half, n, last=False):
                nj, block_n = len(J_OF[half]), NB * half + n
                done = len(J_OF[0]) * NB * half + nj * n
                level = [0]

                def some(k):
                    if half:
                        return
                    for i in range(level[0], min(level[0] + k, LEVELS)):
                        if i == 0:
                            act.wait_ge(s_bnorm, n + 1)
                        wait(act, s_bacc, LEVELS * n + i - NYB + 1)
                        act.activation(nb_y[:, i % NYB], nb_w[:], ACT.Identity,
                                       bias=bound_b[:, i:i + 1], scale=STEEP).then_inc(s_by, 1)
                    level[0] = min(level[0] + k, LEVELS)

                def high(j):
                    act.wait_ge(s_hid, done + j + 1)
                    if j == 0:
                        wait(act, s_down, NT * block_n)
                    act.activation(hid_h[:, j], hid[:, j % 2], ACT.Copy).then_inc(s_hh, 1)

                if not half:
                    load_b(n)
                for j in range(nj):
                    act.wait_ge(s_gu, done + j + 1)
                    wait(act, s_hl, done + j - 1)
                    wait(act, s_hh, done + j - 1)
                    act.activation(silu[:, j % 2], gu(j)[:, 0:TB], ACT.Silu).then_inc(s_silu, 1)
                    if j:
                        high(j - 1)
                    if 1 < j < nj - 1:
                        some(2)
                high(nj - 1)
                if not last:
                    split(block_n + 1, done + nj)
                some(LEVELS)
                for k in range(NT):
                    if half:
                        act.wait_ge(s_nmr2, NT * n + k + 1)
                        act.activation(o_tok[:, k], o_tok[:, k], ACT.Identity,
                                       bias=nmr2[:, k:k + 1], scale=rstd2[:, k:k + 1]).then_inc(s_o, 1)
                    else:
                        act.wait_ge(s_down, NT * n + k + 1)
                        act.activation(part[:, bass.ds(NT * n + k, 1), :].rearrange("p a e -> p (a e)"),
                                       ps_c[:, k], ACT.Copy).then_inc(s_part, 1)

            prepare(0)
            split(0, 0)
            ffn(0, 0)
            with act.Fori(1, NB) as n:
                ffn(0, n)
            prepare(1)
            with act.Fori(0, NB - 1) as n:
                ffn(1, n)
            ffn(1, NB - 1, last=True)

        @block.tensor
        def _(pe):
            pe.wait_ge(s_const, N_CONST + 2)
            for i in range(3):
                pe.wait_ge(s_wload[i], 16)
                for c in range(KC):
                    wait(pe, s_wl, i * KC + c - 1)
                    for m in range(KC):
                        t = pe.transpose(ps_s[:, (i * KC + c) % 2, m * P:(m + 1) * P],
                                         wst[:, i % 2, m, c * P:(c + 1) * P], ident[:])
                    t.then_inc(s_wtr, 1)
            pe.wait_ge(s_wl, 3 * KC)
            pe.wait_ge(s_wh, 3 * KC)

            def three(dst, wh, wl, rh, rl, start, stop, skip=False):
                pe.matmul(dst, wh, rh, start=start, stop=False, skip_group_check=skip)
                pe.matmul(dst, wh, rl, start=False, stop=False, skip_group_check=skip)
                return pe.matmul(dst, wl, rh, start=False, stop=stop, skip_group_check=skip)

            def body(n, proj, att, ln):
                def scores(g):
                    b = n - 1
                    if not att:
                        return
                    wait(pe, s_ssub, NG * b + g - 1)
                    for i in range(GI):
                        for q in range(Q4):
                            s = q * TI + g * GI + i
                            t = pe.matmul(ps_s[32 * q:32 * q + 32, g % 2, i * H:(i + 1) * H],
                                          q_st[:, :, s], k_st[:, :, s], start=True, stop=True)
                    t.then_inc(s_score, 1)

                def project(u):
                    if not proj:
                        return
                    i, half = divmod(u, 2)
                    wait(pe, s_evac, 6 * n + u - 1)
                    for a in range(2):
                        m = 2 * half + a
                        for c in range(KC):
                            t = three(ps_a[:, u % 2, a * TB:a * TB + TB],
                                      w_h[:, i, c, m * P:(m + 1) * P], w_l[:, i, c, m * P:(m + 1) * P],
                                      x_h[:, c], x_l[:, c], c == 0, c == KC - 1)
                    t.then_inc(s_proj, 1)

                if proj:
                    pe.wait_ge(s_x, 16 * (n + 1))
                    wait(pe, s_xT, n)
                    for c in range(KC):
                        for k in range(NT):
                            t = pe.transpose(ps_t[:].rearrange("p a b -> p (a b)")[:, c * TB + k * P:c * TB + k * P + P],
                                             x_tok[:, k, c * P:(c + 1) * P], ident[:])
                    t.then_inc(s_xtr, 1)
                if att:
                    pe.wait_ge(s_ld_stack, 16 * 12 * n)
                scores(0)
                scores(1)
                if proj:
                    pe.wait_ge(s_xh, n + 1)
                    pe.wait_ge(s_xl, n + 1)
                project(0)
                project(1)
                scores(2)
                project(2)
                scores(3)
                for u in (3, 4, 5):
                    project(u)
                if ln:
                    pe.wait_ge(s_y, n - 1)
                    if proj:
                        pe.wait_ge(s_xT, n + 1)
                    for c in range(KC):
                        t = pe.matmul(ps_t[:, 0, 0:TB], mean_w[:], y1[:, c], start=(c == 0), stop=(c == KC - 1))
                    t.then_inc(s_mean, 1)
                if att:
                    b = n - 1
                    pe.wait_ge(s_ld_v, 16 * Q4 * (b + 1))
                    for g in range(NG):
                        pe.wait_ge(s_probT, NG * b + g + 1)
                        wait(pe, s_ctx, NG * b + g - 1)
                        for i in range(GI):
                            at = g * GI + i
                            t = pe.matmul(ps_c[0:Q4 * D, g % 2, i * H:(i + 1) * H],
                                          v_bd[:].rearrange("p a d i -> p (a d) i")[:, :, at],
                                          probT[:, at], start=True, stop=True)
                        t.then_inc(s_pv, 1)
                if ln:
                    pe.wait_ge(s_sq, n - 1)
                    for k in range(NT):
                        for c in range(KC):
                            t = pe.matmul(ps_t[:, 1, k:k + 1], sq1[:, c, k * P:(k + 1) * P], mean_w[:, 0:1],
                                          start=(c == 0), stop=(c == KC - 1))
                    t.then_inc(s_var, 1)
                    pe.wait_ge(s_diag, n - 1)
                    for k in range(NT):
                        t = pe.matmul(ps_t[:, 0, k * P:(k + 1) * P], ones[:], diag1[:, k], start=True, stop=True)
                    t.then_inc(s_spread, 1)
                    pe.wait_ge(s_x1, n - 1)

            iterations(pe, body)
            phase_1_over(pe)

            def prepare(half):
                for i in PREP_OF[half]:
                    pe.wait_ge(s_stg[prep_slot[i]], 16 * prep_count[i])
                    wait(pe, s_fl, i - 3)
                    if half and i - PREP_OF[1][0] < 4:
                        pe.wait_ge(s_hid, len(J_OF[0]) * NB)
                    for c in range(KC):
                        t = pe.transpose(prep_bank(i)[:, c * P:(c + 1) * P], stg[:, prep_slot[i], c], ident[:])
                    t.then_inc(s_ftr, 1)
                pe.wait_ge(s_fh, PREP_OF[half][-1] + 1)
                pe.wait_ge(s_fl, PREP_OF[half][-1] + 1)

            def ffn(half, n):
                nj, block_n = len(J_OF[half]), NB * half + n
                done = len(J_OF[0]) * NB * half + nj * n
                pe.wait_ge(s_x1h, block_n + 1)
                pe.wait_ge(s_x1l, block_n + 1)
                for j, chunk in enumerate(J_OF[half]):
                    cols = slice(chunk * P, (chunk + 1) * P)
                    wait(pe, s_hid, done + j - 3 if j > 3 else done)
                    for w in range(2):
                        for c in range(KC):
                            t = three(gu(j)[:, w * TB:(w + 1) * TB], f1_h[:, w, c, cols], f1_l[:, w, c, cols],
                                      x1_h[:, c], x1_l[:, c], c == 0, c == KC - 1)
                    t.then_inc(s_gu, 1)
                    if not half and j == nj // 2:
                        for k in range(NT):
                            wait(pe, s_part, NT * (n - 1) + k + 1)
                            for c in range(KC):
                                for x_part in (x1_h, x1_l):
                                    pe.matmul(ps_c[:, k, c * P:(c + 1) * P], x_part[:, c, k * P:(k + 1) * P],
                                              ident_r[:], start=(c == 0 and x_part is x1_h), stop=False,
                                              skip_group_check=True)
                for k in range(NT):
                    tok = slice(k * P, (k + 1) * P)
                    if half:
                        wait(pe, s_sum, NT * (n - 1) + k + 1)
                    for j, chunk in enumerate(J_OF[half]):
                        if k == 0:
                            pe.wait_ge(s_hh, done + j + 1)
                            pe.wait_ge(s_hl, done + j + 1)
                        t = three(ps_c[:, k], hid_h[:, j, tok], hid_l[:, j, tok], f3_h[:, chunk], f3_l[:, chunk],
                                  half == 1 and j == 0, j == nj - 1, skip=not half)
                    t.then_inc(s_down, 1)

            pe.wait_ge(s_identr, 1)
            prepare(0)
            ffn(0, 0)
            with pe.Fori(1, NB) as n:
                ffn(0, n)
            prepare(1)
            pe.wait_ge(s_part, NT * NB)
            ffn(1, 0)
            with pe.Fori(1, NB) as n:
                ffn(1, n)

        @block.vector
        def _(dve):
            for i in range(3 * KC):
                dve.wait_ge(s_wh, i + 1)
                dve.tensor_tensor(w_l[:, i // KC, i % KC], ps_s[:, i % 2], w_h[:, i // KC, i % KC].bitcast(F32),
                                  ALU.subtract).then_inc(s_wl, 1)

            def body(n, proj, att, ln):
                def scales():
                    dve.wait_ge(s_nld, 3 * 16 * (n + 1))
                    wait(dve, s_nscale, n)
                    dve.tensor_reduce(nf_max[:], blocks_of(nf_raw[:]), AX.X, ALU.max, apply_absolute_value=True
                                      ).then_inc(s_nmax, 1)
                    dve.wait_ge(s_nmax, n + 1)
                    dve.tensor_scalar(nf_den[:], nf_max[:], TINY, None, ALU.max).then_inc(s_nden, 1)
                    dve.wait_ge(s_nden, n + 1)
                    wait(dve, s_nnorm, 2 * n)
                    dve.reciprocal(nf_rec[:], nf_den[:]).then_inc(s_nrec, 1)

                def lift(lo, hi, unit):
                    for step in range(lo, hi):
                        i, c = divmod(step, 2)
                        at = STEPS * unit + step
                        a, b = CHAINS[c]
                        y, acc = nf_y[:, step % NY, 0:b - a], nf_acc[:, a:b]
                        if step == 0:
                            wait(dve, s_nst, 3 * 16 * unit)
                        dve.wait_ge(s_ny, at + 1)
                        if i == 0:
                            dve.tensor_scalar(acc, y, float(NF4[1]), float(NF4[0]), ALU.min, ALU.max
                                              ).then_inc(s_nacc, 1)
                        else:
                            dve.wait_ge(s_nacc, at - 1)
                            dve.scalar_tensor_tensor(out=acc, in0=y, scalar=float(NF4[i + 1]), in1=acc,
                                                     op0=ALU.min, op1=ALU.max).then_inc(s_nacc, 1)

                step = [0]

                def some(k):
                    if proj:
                        hi = min(step[0] + k, STEPS - LATE)
                        lift(step[0], hi, n)
                        step[0] = hi

                b = n - 1

                def part_of(t, g):
                    return t[:, g * GI:(g + 1) * GI]

                def wide(t, g):
                    return part_of(t, g).unsqueeze(2).to_broadcast([P, GI, H])

                def biggest(g):
                    dve.wait_ge(s_score, NG * b + g + 1)
                    dve.tensor_reduce(part_of(smax, g), scores_of(g), AX.X, ALU.max).then_inc(s_smax, 1)

                def scores_of(g):
                    return ps_s[:, g % 2].rearrange("p (i t) -> p i t", t=H)

                def shift(g):
                    dve.wait_ge(s_smax, NG * b + g + 1)
                    dve.tensor_tensor(part_of(prob, g), scores_of(g), wide(smax, g), ALU.subtract
                                      ).then_inc(s_ssub, 1)

                def total(g):
                    dve.wait_ge(s_exp, NG * b + g + 1)
                    dve.tensor_reduce(part_of(ssum, g), part_of(prob, g), AX.X, ALU.add).then_inc(s_ssum, 1)

                def invert(g):
                    dve.wait_ge(s_ssum, NG * b + g + 1)
                    dve.reciprocal(part_of(srec, g), part_of(ssum, g)).then_inc(s_srec, 1)

                def normalise(g):
                    dve.wait_ge(s_srec, NG * b + g + 1)
                    dve.tensor_tensor(part_of(prob, g), part_of(prob, g), wide(srec, g), ALU.mult
                                      ).then_inc(s_norm, 1)

                def turn(g):
                    dve.wait_ge(s_norm, NG * b + g + 1)
                    if g == 0:
                        wait(dve, s_pv, NG * b)
                    dve.transpose(part_of(probT, g).rearrange("p i h -> p (i h)"),
                                  part_of(prob, g).rearrange("p i h -> p (i h)")).then_inc(s_probT, 1)

                def softmax():
                    for step, g in ((biggest, 0), (biggest, 1), (shift, 0), (shift, 1),
                                    (total, 0), (biggest, 2), (invert, 0), (shift, 2), (normalise, 0),
                                    (total, 1), (turn, 0), (biggest, 3), (invert, 1), (shift, 3), (normalise, 1),
                                    (total, 2), (turn, 1), (invert, 2), (total, 3), (normalise, 2),
                                    (invert, 3), (turn, 2), (normalise, 3)):
                        step(g)
                    if proj:
                        some(1)
                    turn(3)

                if proj:
                    scales()
                if att:
                    lift(STEPS - LATE, STEPS, n - 1)
                if att:
                    softmax()
                some(6)
                if ln:
                    dve.wait_ge(s_mean, n - 1)
                    dve.tensor_tensor(y1[:], y1[:], ps_t[:, 0, 0:TB].unsqueeze(1).to_broadcast([P, KC, TB]),
                                      ALU.subtract).then_inc(s_cen, 1)
                some(8)
                if ln:
                    dve.wait_ge(s_var, n - 1)
                    dve.tensor_scalar(ve1[:], ps_t[:, 1, 0:NT], EPS, None, ALU.add).then_inc(s_ve, 1)
                some(2)
                if ln:
                    dve.wait_ge(s_spread, n - 1)
                    dve.tensor_tensor(y1[:], y1[:], ps_t[:, 0, 0:TB].unsqueeze(1).to_broadcast([P, KC, TB]),
                                      ALU.mult).then_inc(s_x1, 1)
                some(STEPS)

            iterations(dve, body)
            phase_1_over(dve)
            dve.memset(stg[:, NS], 0.0).then_inc(s_pad, 1)

            def prepare(half):
                for i in PREP_OF[half]:
                    w, j = prep[i]
                    dve.wait_ge(s_fh, i + 1)
                    src = prep_bank(i)
                    if w < 2:
                        at = (slice(None), w, slice(None), slice(j * P, (j + 1) * P))
                        hi, lo = f1_h[at], f1_l[at]
                        src = src.rearrange("p (c k) -> p c k", c=KC)
                    else:
                        hi, lo = f3_h[:, j], f3_l[:, j]
                    dve.tensor_tensor(lo, src, hi.bitcast(F32), ALU.subtract).then_inc(s_fl, 1)

            def split(block_n, done):
                dve.wait_ge(s_x1h, block_n + 1)
                wait(dve, s_gu, done)
                dve.tensor_tensor(x1_l[:], x1[:], x1_h[:].bitcast(F32), ALU.subtract).then_inc(s_x1l, 1)

            def ffn(half, n, last=False):
                nj, block_n = len(J_OF[half]), NB * half + n
                done = len(J_OF[0]) * NB * half + nj * n
                level = [0]

                def some(k):
                    if half:
                        return
                    for i in range(level[0], min(level[0] + k, LEVELS)):
                        if i == 0:
                            wait(dve, s_bst, 2 * 16 * n)
                        dve.wait_ge(s_by, LEVELS * n + i + 1)
                        y = nb_y[:, i % NYB]
                        if i == 0:
                            dve.tensor_scalar(nb_acc[:], y, float(NF4[1]), float(NF4[0]), ALU.min, ALU.max
                                              ).then_inc(s_bacc, 1)
                        else:
                            dve.wait_ge(s_bacc, LEVELS * n + i)
                            dve.scalar_tensor_tensor(out=nb_acc[:], in0=y, scalar=float(NF4[i + 1]), in1=nb_acc[:],
                                                     op0=ALU.min, op1=ALU.max).then_inc(s_bacc, 1)
                    level[0] = min(level[0] + k, LEVELS)

                def low(j):
                    dve.wait_ge(s_hh, done + j + 1)
                    dve.tensor_tensor(hid_l[:, j], hid[:, j % 2], hid_h[:, j].bitcast(F32), ALU.subtract
                                      ).then_inc(s_hl, 1)

                def scales_b():
                    dve.wait_ge(s_bld, 2 * 16 * (n + 1))
                    wait(dve, s_bdq, n)
                    dve.tensor_reduce(nb_max[:], blocks_of(nb_w[:]), AX.X, ALU.max, apply_absolute_value=True
                                      ).then_inc(s_bmax, 1)
                    dve.wait_ge(s_bmax, n + 1)
                    dve.tensor_scalar(nb_den[:], nb_max[:], TINY, None, ALU.max).then_inc(s_bden, 1)
                    dve.wait_ge(s_bden, n + 1)
                    dve.reciprocal(nb_rec[:], nb_den[:]).then_inc(s_brec, 1)

                for j in range(nj):
                    dve.wait_ge(s_silu, done + j + 1)
                    dve.tensor_tensor(hid[:, j % 2], silu[:, j % 2], gu(j)[:, TB:2 * TB], ALU.mult
                                      ).then_inc(s_hid, 1)
                    if j:
                        low(j - 1)
                    if j == 1 and not half:
                        scales_b()
                    if 1 < j < nj - 1:
                        some(2)
                low(nj - 1)
                if not last:
                    split(block_n + 1, done + nj)
                some(LEVELS)
                if not half:
                    return
                for k in range(NT):
                    at = NT * n + k + 1
                    dve.wait_ge(s_down, NT * NB + at)
                    wait(dve, s_out[k], 16 * n)
                    dve.tensor_tensor(o_tok[:, k], ps_c[:, k],
                                      part[:, bass.ds(NT * n + k, 1), :].rearrange("p a e -> p (a e)"), ALU.add
                                      ).then_inc(s_sum, 1)
                    dve.wait_ge(s_sum, at)
                    dve.bn_stats(st6[:, k], o_tok[:, k]).then_inc(s_bn, 1)
                    hold(dve, s_bn, at)
                    dve.bn_aggr(mv[:, k], st6[:, k]).then_inc(s_mv, 1)
                    dve.wait_ge(s_mv, at)
                    dve.tensor_scalar(ve2[:, k:k + 1], mv[:, k, 1:2], EPS, None, ALU.add).then_inc(s_ve2, 1)
                    dve.wait_ge(s_rstd2, at)
                    wait(dve, s_o, at - NT)
                    dve.scalar_tensor_tensor(out=nmr2[:, k:k + 1], in0=mv[:, k, 0:1], scalar=-1.0,
                                             in1=rstd2[:, k:k + 1], op0=ALU.mult, op1=ALU.mult
                                             ).then_inc(s_nmr2, 1)

            prepare(0)
            split(0, 0)
            ffn(0, 0)
            with dve.Fori(1, NB) as n:
                ffn(0, n)
            prepare(1)
            ffn(1, 0)
            with dve.Fori(1, NB - 1) as n:
                ffn(1, n)
            ffn(1, NB - 1, last=True)


_INS = ["L0_attn_hidden_states", "L0_attn_wq", "L0_attn_bq", "L0_attn_wk", "L0_attn_bk", "L0_attn_wv",
        "L0_attn_bv", "L0_ffn_w1", "L0_ffn_w2", "L0_ffn_w3"]


def kernel(**inputs):
    import concourse.bacc as _bacc
    from concourse.bass_utils import run_bass_kernel_spmd as _run

    nc = _bacc.Bacc("TRN2", target_bir_lowering=False, num_devices=1)
    arrays, args = {}, []
    for name in _INS:
        a = np.ascontiguousarray(inputs[name])
        arrays[f"in_{name}"] = a
        args.append(nc.dram_tensor(f"in_{name}", a.shape, mybir.dt.from_np(a.dtype), kind="ExternalInput").ap())
    shape = inputs["L0_attn_hidden_states"].shape
    args.append(nc.dram_tensor("out_0", shape, F32, kind="ExternalOutput").ap())
    layer_kernel(nc, *args)
    r = _run(nc, [arrays], core_ids=[0])
    return r.results[0]["out_0"]
```

```python
from contextlib import ExitStack

import numpy as np

import concourse.bass as bass
from concourse import mybir

F32 = mybir.dt.float32
F32R = mybir.dt.float32r
BF16 = mybir.dt.bfloat16
ALU = mybir.AluOpType
ACT = mybir.ActivationFunctionType
AX = mybir.AxisListType

P = 128
NF4 = np.array([-1.0, -0.6961928009986877, -0.5250730514526367, -0.39491748809814453,
                -0.28444138169288635, -0.18477343022823334, -0.09105003625154495, 0.0,
                0.07958029955625534, 0.16093020141124725, 0.24611230194568634,
                0.33791524171829224, 0.44070982933044434, 0.5626170039176941,
                0.7229568362236023, 1.0], dtype=np.float32)
BOUNDS = (NF4[:-1] + NF4[1:]) * np.float32(0.5)
LEVELS = len(BOUNDS)
QBLOCK = 64
EPS = 1e-5
TINY = 1.2e-38
STEEP = float(2.0 ** 64)


def level_bound(i):
    b = BOUNDS[i]
    return float(b if NF4[i + 1] > 0 else np.nextafter(b, np.float32(2.0), dtype=np.float32))


def layer_kernel(nc, x, wq, bq, wk, bk, wv, bv, w1, w2, w3, out):
    B, S, E = x.shape
    T = B * S
    KC = E // P
    H, D = 32, 16
    HID = w1.shape[0]
    NJ = -(-HID // P)
    HLAST = HID - (NJ - 1) * P
    TB = 256
    NB = T // TB
    NT = TB // P
    Q4 = 4
    TI = TB // Q4
    GI = 16
    NG = TI // GI
    Q_TERMS = [0, 0, 0, 1, 1, 2]
    K_TERMS = [0, 1, 2, 0, 1, 0]
    KS = D * len(Q_TERMS)
    JA = 5
    J_OF = [range(JA), range(JA, NJ)]
    BLOCKS_A = JA * P * E // (P * QBLOCK)
    BLOCKS_B = (HID - JA * P) * E // (P * QBLOCK)
    BLOCKS_3 = HID * E // (P * QBLOCK)
    NA, N_B, N3 = (-(-b // NB) for b in (BLOCKS_A, BLOCKS_B, BLOCKS_3))
    NJH = max(len(js) for js in J_OF)
    QN = 2 * NA + N3
    FA, FB = NA * QBLOCK, N_B * QBLOCK
    LATE = 2
    FIRST_B = (5, 4, 6)
    N_CONST = 5
    NY, NYF, NYB = 3, 2, 3

    xf = x.rearrange("b s e -> (b s) e")
    of = out.rearrange("b s e -> (b s) e")
    flat = [w.rearrange("a b -> (a b)") for w in (w1, w2, w3)]

    qk_d = nc.dram_tensor("qk_parts", [2, 3, E, T], BF16, kind="Internal").ap()
    v_d = nc.dram_tensor("v_feature_major", [E, T], F32, kind="Internal").ap()
    xT_d = nc.dram_tensor("x_feature_major", [E, T], F32, kind="Internal").ap()
    ctx_d = nc.dram_tensor("context_feature_major", [E, T], F32, kind="Internal").ap()
    x1_d = nc.dram_tensor("x1_feature_major", [E, T], F32, kind="Internal").ap()
    dq_d = nc.dram_tensor("dequantised", [3, HID * E], F32, kind="Internal").ap()

    def features(t, t0, n=TB):
        return t.rearrange("(c p) t -> p c t", p=P)[:, :, bass.ds(t0, n)]

    with ExitStack() as both, ExitStack() as first:
        def sb(name, shape, dt, stack=first):
            return stack.enter_context(nc.sbuf_tensor(name, shape, dt))

        def sem(name):
            return both.enter_context(nc.semaphore(name))

        def bank(name, n):
            return both.enter_context(nc.psum_tensor(name, [P, n, 512], F32))

        ident = sb("ident", [P, P], F32, both)
        ident_r = sb("ident_r", [P, P], F32R, both)
        unit = sb("unit", [P, QN], F32, both)
        half_neg = sb("half_neg", [P, NT], F32, both)
        bound_b = sb("bound_b", [P, LEVELS], F32, both)

        part = sb("part", [P, T // P, E], F32, both)

        def in_part(lo, hi):
            return part[:, lo:hi].rearrange("p a e -> p (a e)")

        ctx = in_part(0, 4)[0:Q4 * D].rearrange("p (h i) -> p h i", h=H)
        y1 = in_part(4, 6).rearrange("p (c t) -> p c t", c=KC)
        ctxT = in_part(6, 8).rearrange("p (c t) -> p c t", c=KC)
        diag1 = in_part(8, 9)[:, 0:NT * P].rearrange("p (k m) -> p k m", k=NT)
        ve1 = in_part(9, 10)[:, 0:NT]
        rstd1 = in_part(9, 10)[:, NT:2 * NT]
        ones = in_part(9, 10)[:, P:2 * P]
        mean_w = in_part(9, 10)[:, 2 * P:3 * P]
        vT = in_part(10, 12).rearrange("p (c t) -> p c t", c=KC)
        x_tok = part[:, 12:14]
        xT = in_part(14, 16).rearrange("p (c t) -> p c t", c=KC)

        first_b = in_part(10, 16)
        fb_w, fb_acc = first_b[:, 0:2 * FB], first_b[:, 2 * FB:4 * FB]
        fb_y = first_b[:, 4 * FB:(4 + 2 * NYF) * FB].rearrange("p (y f) -> p y f", y=NYF)

        w_h = sb("w_h", [P, 3, KC, E], F32R)
        w_l = sb("w_l", [P, 3, KC, E], F32R)
        bias = sb("bias", [P, 3, KC], F32)
        x_h = sb("x_h", [P, KC, TB], F32R)
        x_l = sb("x_l", [P, KC, TB], F32R)
        qk = sb("qk", [P, 2, KC, TB], F32)
        qk_part = sb("qk_part", [P, 2, 3, KC * TB], BF16)
        q_st = sb("q_st", [KS, H, TB], BF16)
        k_st = sb("k_st", [KS, H, TB], BF16)
        v_bd = sb("v_bd", [P, Q4, D, TI], F32)
        prob2 = sb("prob2", [P, 2, TI, H], F32)
        prob, probT = prob2[:, 0], prob2[:, 1]
        smax = sb("smax", [P, TI], F32)
        ssum = sb("ssum", [P, TI], F32)
        srec = sb("srec", [P, TI], F32)
        sq1 = ctxT
        nf_raw = sb("nf_raw", [P, QN * QBLOCK], F32)
        nf_w = sb("nf_w", [P, QN * QBLOCK], F32)
        nf_acc = sb("nf_acc", [P, QN * QBLOCK], F32)
        nf_y = sb("nf_y", [P, NY, QN * QBLOCK], F32)
        nf_max = sb("nf_max", [P, QN], F32)
        nf_den = sb("nf_den", [P, QN], F32)
        nf_rec = sb("nf_rec", [P, QN], F32)
        nf_scale = sb("nf_scale", [P, QN], F32)
        wst = prob2[:].rearrange("p a i h -> p a (i h)").rearrange("p a (m e) -> p a m e", e=E)

        first.close()

        f1_h = sb("f1_h", [P, 2, KC, NJ * P], F32R, both)
        f1_l = sb("f1_l", [P, 2, KC, NJ * P], F32R, both)
        f3_h = sb("f3_h", [P, NJ, E], F32R, both)
        f3_l = sb("f3_l", [P, NJ, E], F32R, both)
        NS = 5
        stg = sb("stg", [P, NS + 1, KC, P], F32, both)
        x1 = sb("x1", [P, KC, TB], F32, both)
        x1_h = sb("x1_h", [P, KC, TB], F32R, both)
        x1_l = sb("x1_l", [P, KC, TB], F32R, both)
        silu = sb("silu", [P, 2, TB], F32, both)
        hid = silu
        hid_h = sb("hid_h", [P, NJH, TB], F32R, both)
        hid_l = sb("hid_l", [P, NJH, TB], F32R, both)
        nb_w = sb("nb_w", [P, 2 * FB], F32, both)
        rest = stg[:].rearrange("p s c k -> p (s c k)")
        nb_y = rest[:, 0:NYB * 2 * FB].rearrange("p (y f) -> p y f", y=NYB)
        nb_acc = rest[:, NYB * 2 * FB:(NYB + 1) * 2 * FB]
        o_tok = rest[:, 0:NT * E].rearrange("p (k e) -> p k e", k=NT)
        nb_max = sb("nb_max", [P, 2 * N_B], F32, both)
        nb_den = sb("nb_den", [P, 2 * N_B], F32, both)
        nb_scale = sb("nb_scale", [P, 2 * N_B], F32, both)
        nb_rec = sb("nb_rec", [P, 2 * N_B], F32, both)
        st6 = sb("st6", [P, 2, 6], F32, both)
        mv = sb("mv", [P, 2, 2], F32, both)
        ve2 = sb("ve2", [P, 2], F32, both)
        rstd2 = sb("rstd2", [P, 2], F32, both)
        nmr2 = sb("nmr2", [P, 2], F32, both)

        ps_t = bank("ps_t", 2)
        ps_a = bank("ps_a", 2)
        ps_s = bank("ps_s", 2)
        ps_c = bank("ps_c", 2)

        s_const = sem("s_const")
        s_identr = sem("s_identr")
        s_bias = sem("s_bias")
        s_wload = [sem(f"s_wload{i}") for i in range(3)]
        s_wtr = sem("s_wtr")
        s_wh = sem("s_wh")
        s_wl = sem("s_wl")
        s_x = sem("s_x")
        s_xtr = sem("s_xtr")
        s_xT = sem("s_xT")
        s_xh = sem("s_xh")
        s_xl = sem("s_xl")
        s_proj = sem("s_proj")
        s_evac = sem("s_evac")
        s_part_h = sem("s_part_h")
        s_part_r = sem("s_part_r")
        s_part_m = sem("s_part_m")
        s_part_l = sem("s_part_l")
        s_st_q = sem("s_st_q")
        s_st_k = sem("s_st_k")
        s_st_v = sem("s_st_v")
        s_st_xT = sem("s_st_xT")
        s_ld_stack = sem("s_ld_stack")
        s_ld_v = sem("s_ld_v")
        s_score = sem("s_score")
        s_smax = sem("s_smax")
        s_ssub = sem("s_ssub")
        s_exp = sem("s_exp")
        s_ssum = sem("s_ssum")
        s_srec = sem("s_srec")
        s_norm = sem("s_norm")
        s_probT = sem("s_probT")
        s_pv = sem("s_pv")
        s_ctx = sem("s_ctx")
        s_st_ctx = sem("s_st_ctx")
        s_ld_ln = sem("s_ld_ln")
        s_y = sem("s_y")
        s_mean = sem("s_mean")
        s_cen = sem("s_cen")
        s_sq = sem("s_sq")
        s_var = sem("s_var")
        s_ve = sem("s_ve")
        s_rstd = sem("s_rstd")
        s_diag = sem("s_diag")
        s_spread = sem("s_spread")
        s_x1 = sem("s_x1")
        s_st_x1 = sem("s_st_x1")
        s_nld = sem("s_nld")
        s_nmax = sem("s_nmax")
        s_nden = sem("s_nden")
        s_nrec = sem("s_nrec")
        s_nscale = sem("s_nscale")
        s_nnorm = sem("s_nnorm")
        s_ny = sem("s_ny")
        s_nacc = sem("s_nacc")
        s_ndq = sem("s_ndq")
        s_nst = sem("s_nst")
        s_bld = sem("s_bld")
        s_bmax = sem("s_bmax")
        s_bden = sem("s_bden")
        s_brec = sem("s_brec")
        s_bnorm = sem("s_bnorm")
        s_bscale = sem("s_bscale")
        s_by = sem("s_by")
        s_bacc = sem("s_bacc")
        s_bdq = sem("s_bdq")
        s_bst = sem("s_bst")
        s_stg = [sem(f"s_stg{i}") for i in range(NS + 1)]
        s_pad = sem("s_pad")
        s_ftr = sem("s_ftr")
        s_fh = sem("s_fh")
        s_fl = sem("s_fl")
        s_x1ld = sem("s_x1ld")
        s_x1h = sem("s_x1h")
        s_x1l = sem("s_x1l")
        s_gu = sem("s_gu")
        s_silu = sem("s_silu")
        s_hid = sem("s_hid")
        s_hh = sem("s_hh")
        s_hl = sem("s_hl")
        s_down = sem("s_down")
        s_part = sem("s_part")
        s_sum = sem("s_sum")
        s_bn = sem("s_bn")
        s_mv = sem("s_mv")
        s_ve2 = sem("s_ve2")
        s_rstd2 = sem("s_rstd2")
        s_nmr2 = sem("s_nmr2")
        s_o = sem("s_o")
        s_out = [sem(f"s_out{k}") for k in range(NT)]

        def wait(eng, s, value):
            if not (isinstance(value, int) and value <= 0):
                eng.wait_ge(s, value)

        def waits(eng, *pairs):
            for s, v in pairs:
                if not isinstance(v, int):
                    eng.compute_val(v)
            for s, v in pairs:
                wait(eng, s, v)

        def hold(eng, s, value):
            eng.wait_ge(s_const, N_CONST)
            wait(eng, s, value)

        def phase_1_over(eng):
            eng.wait_ge(s_st_x1, 16 * NB)
            eng.wait_ge(s_nst, 3 * 16 * NB)

        def attention_over(eng):
            eng.wait_ge(s_pv, NG * NB)
            eng.wait_ge(s_nst, 3 * 16 * NB)

        def first_block(n):
            return isinstance(n, int) and n == 0

        def iterations(eng, body, between=lambda: None):
            body(0, True, False, False)
            body(1, True, True, False)
            with eng.Fori(2, NB) as n:
                body(n, True, True, True)
            body(NB, False, True, True)
            body(NB + 1, False, False, True, between)

        def start_of(n, count, blocks):
            lap = count * NB - blocks
            return 0 if isinstance(n, int) and n == 0 else (n * count - lap) * QBLOCK

        def rows_view(t, lo, hi):
            return t[lo * E:hi * E].rearrange("(p f) -> p f", p=P)

        PARTS = [(rows_view(flat[w], 0, hi), rows_view(dq_d[w], 0, hi), blocks, count, col)
                 for w, hi, blocks, count, col in ((0, JA * P, BLOCKS_A, NA, 0), (1, JA * P, BLOCKS_A, NA, FA),
                                                   (2, HID, BLOCKS_3, N3, 2 * FA))]
        PARTS_B = [(rows_view(flat[w], JA * P, HID), rows_view(dq_d[w], JA * P, HID), w * FB) for w in range(2)]

        def blocks_of(t):
            return t.rearrange("p (b k) -> p b k", k=QBLOCK)

        def slice_buffers(n):
            return (fb_w, fb_acc, fb_y, NYF) if isinstance(n, int) and n == 0 else (nb_w[:], nb_acc, nb_y, NYB)

        def gu(j):
            return (ps_a, ps_s)[(j // 2) % 2][:, j % 2]

        block = both.enter_context(nc.Block())

        prep = [(w, j) for j in J_OF[0] for w in range(3)]
        whole = J_OF[1][:-1]
        prep += [(2, j) for j in whole] + [(w, j) for j in whole for w in range(2)]
        for w in range(3):
            prep.insert(3 * JA + 4 + 4 * w, (2 - w, NJ - 1))
        prep_slot = []
        prep_count = []
        used = [0] * (NS + 1)
        turn = 0
        for w, j in prep:
            if j == NJ - 1:
                s = NS
            else:
                s = turn % NS
                turn += 1
            prep_slot.append(s)
            used[s] += 1
            prep_count.append(used[s])

        def prep_bank(i):
            return ps_s[:, i % 2] if i % 4 < 2 else ps_a[:, i % 2]

        prep_prev = []
        for i, s in enumerate(prep_slot):
            before = [k for k in range(i) if prep_slot[k] == s]
            prep_prev.append(before[-1] + 1 if before else 0)

        @block.sync
        def _(sp):
            def token(v):
                if not isinstance(v, int):
                    for size in (1, 2, 4):
                        sp.compute_val(v * size)
                return v

            def places(n):
                at = [start_of(n, count, blocks) for _, _, blocks, count, _ in PARTS]
                for v in at:
                    if not isinstance(v, int):
                        sp.compute_val(v * 4)
                return at

            def load_x(n):
                t0 = token(n * TB)
                wait(sp, s_xtr, n)
                sp.dma_start(x_tok[:], xf[bass.ds(t0, TB), :].rearrange("(k p) e -> p k e", p=P)
                             ).then_inc(s_x, 16)

            def load_slice(n):
                at = places(n)
                wait(sp, s_nnorm, n)
                for w, (src, _, _, count, col) in enumerate(PARTS):
                    sp.dma_start(nf_raw[:, col:col + count * QBLOCK],
                                 src[:, bass.ds(at[w], count * QBLOCK)]).then_inc(s_nld, 16)

            def body(n, between=lambda: None):
                known = isinstance(n, int)
                proj, before = not known or n < NB, not known or 1 <= n <= NB
                ln, tail = not known or 2 <= n <= NB + 1, not known or n >= 3

                def token(v):
                    if not known:
                        for size in (1, 2, 4):
                            sp.compute_val(v * size)
                    return v

                if ln:
                    m = n - 2
                    tm = [token(m * TB + q * TI) for q in range(Q4)]
                    wait(sp, s_ctx, NG * (m + 1))
                    for q in range(Q4):
                        sp.dma_start(ctx_d.rearrange("(h d) s -> d h s", d=D)[:, :, bass.ds(tm[q], TI)],
                                     ctx[D * q:D * q + D]).then_inc(s_st_ctx, 16)
                    between()
                if tail:
                    t0 = token((n - 3) * TB)
                    wait(sp, s_x1, n - 2)
                    sp.dma_start(features(x1_d, t0), y1[:]).then_inc(s_st_x1, 16)
                if before:
                    t0 = [token((n - 1) * TB + q * TI) for q in range(Q4)]
                    waits(sp, (s_pv, NG * (n - 1)), (s_st_v, 16 * n))
                    for q in range(Q4):
                        sp.dma_start(v_bd[32 * q:32 * q + 32, q],
                                     v_d.rearrange("(t d) s -> t d s", d=D)[:, :, bass.ds(t0[q], TI)]
                                     ).then_inc(s_ld_v, 16)
                if ln:
                    waits(sp, (s_var, m), (s_st_ctx, 16 * Q4 * (m + 1)))
                    sp.dma_start(ctxT[:], features(ctx_d, tm[0])).then_inc(s_ld_ln, 16)
                    wait(sp, s_st_x1, 16 * m)
                    sp.dma_start(y1[:], features(xT_d, tm[0])).then_inc(s_ld_ln, 16)
                if before:
                    at = places(n - 1)
                    wait(sp, s_ndq, n)
                    for w, (_, dst, _, count, col) in enumerate(PARTS):
                        sp.dma_start(dst[:, bass.ds(at[w], count * QBLOCK)],
                                     nf_acc[:, col:col + count * QBLOCK]).then_inc(s_nst, 16)
                if proj:
                    t0 = token(n * TB)
                    wait(sp, s_xT, n + 1)
                    sp.dma_start(features(xT_d, t0), xT[:]).then_inc(s_st_xT, 16)
                    if not known or n + 1 < NB:
                        load_x(n + 1)
                        load_slice(n + 1)
                    t0 = token(n * TB)
                    for i, s_st in enumerate((s_st_q, s_st_k)):
                        wait(sp, s_part_l, 2 * n + i + 1)
                        for part in range(3):
                            sp.dma_start(features(qk_d[i, part], t0),
                                         qk_part[:, i, part].rearrange("p (c t) -> p c t", c=KC)
                                         ).then_inc(s_st, 16)
                    for i, (stack, terms, s_st) in enumerate(((q_st, Q_TERMS, s_st_q), (k_st, K_TERMS, s_st_k))):
                        waits(sp, (s_st, 3 * 16 * (n + 1)), (s_score, NG * n))
                        for r, part in enumerate(terms):
                            sp.dma_start(stack[D * r:D * r + D],
                                         qk_d[i, part].rearrange("(h d) s -> d h s", d=D)[:, :, bass.ds(t0, TB)]
                                         ).then_inc(s_ld_stack, 16)
                        if i == 0:
                            wait(sp, s_evac, 6 * (n + 1))
                            sp.dma_start(features(v_d, t0), vT[:]).then_inc(s_st_v, 16)

            for i, w in enumerate((wq, wk, wv)):
                if i == 2:
                    sp.wait_ge(s_wtr, KC)
                if i == 1:
                    load_x(0)
                if i == 2:
                    load_slice(0)
                sp.dma_start(wst[:, i % 2], w.rearrange("(m p) e -> p m e", p=P)).then_inc(s_wload[i], 16)
            for i, v in enumerate((bq, bk, bv)):
                sp.dma_start(bias[:, i, :], v.rearrange("(c p) -> p c", p=P), allow_slow_non_contiguous=True
                             ).then_inc(s_bias, 16)

            for n in range(3):
                body(n)
            with sp.Fori(3, NB - 1) as n:
                body(n)
            for n in range(NB - 1, NB + 1):
                body(n)

            staged = [0]

            def stage(stages):
                lo = staged[0]
                staged[0] = hi = min(lo + stages, len(prep))
                for i in range(lo, hi):
                    w, j = prep[i]
                    wait(sp, s_ftr, prep_prev[i])
                    rows = HLAST if j == NJ - 1 else P
                    s = prep_slot[i]
                    if s == NS:
                        sp.wait_ge(s_pad, 1)
                    if w < 2:
                        view = dq_d[w].rearrange("(h e) -> h e", e=E)[j * P:j * P + rows, :]
                        sp.dma_start(stg[0:rows, s].rearrange("p c k -> p (c k)"), view).then_inc(s_stg[s], 16)
                    else:
                        view = dq_d[w].rearrange("(c p h) -> p c h", p=P, h=HID)[:, :, j * P:j * P + rows]
                        sp.dma_start(stg[:, s, :, 0:rows], view).then_inc(s_stg[s], 16)

            def known(n):
                return isinstance(n, int)

            def offset(v):
                if not known(v):
                    sp.compute_val(v * 4)
                return v

            def load_x1(half, n):
                t0 = offset(n * TB)
                wait(sp, s_x1l, NB * half + n)
                sp.dma_start(x1[:], features(x1_d, t0)).then_inc(s_x1ld, 16)

            def load_slice_b(n):
                at = offset(start_of(n, N_B, BLOCKS_B))
                if not (known(n) and n == 1):
                    wait(sp, s_by, LEVELS * n)
                for src, _, col in PARTS_B:
                    sp.dma_start(slice_buffers(n)[0][:, col:col + FB], src[:, bass.ds(at, FB)]).then_inc(s_bld, 16)

            def store_slice(n):
                at = offset(start_of(n, N_B, BLOCKS_B))
                wait(sp, s_bdq, n + 1)
                for _, dst, col in PARTS_B:
                    sp.dma_start(dst[:, bass.ds(at, FB)], slice_buffers(n)[1][:, col:col + FB]).then_inc(s_bst, 16)

            def store(n):
                for k in range(NT):
                    t0 = offset(n * TB + k * P)
                    wait(sp, s_o, NT * n + k + 1)
                    sp.dma_start(of[bass.ds(t0, P), :], o_tok[:, k]).then_inc(s_out[k], 16)

            def begin():
                attention_over(sp)
                load_slice_b(0)
                load_x1(0, 0)
                stage(2 * NS)

            body(NB + 1, begin)
            stage(3 * JA - 2 * NS)
            load_slice_b(1)
            load_x1(0, 1)
            store_slice(0)
            body(NB + 2)
            with sp.Fori(1, NB - 1) as n:
                load_x1(0, n + 1)
                load_slice_b(n + 1)
                store_slice(n)
            load_x1(1, 0)
            store_slice(NB - 1)
            phase_1_over(sp)
            sp.wait_ge(s_bst, 2 * 16 * NB)
            stage(len(prep))
            load_x1(1, 1)
            store(0)
            with sp.Fori(2, NB) as n:
                load_x1(1, n)
                store(n - 1)
            store(NB - 1)
            for k in range(NT):
                sp.wait_ge(s_out[k], 16 * NB)

        @block.gpsimd
        def _(pool):
            pool.memset(ident[:], 0.0).then_inc(s_const, 1)
            pool.memset(mean_w[:], 1.0 / E).then_inc(s_const, 1)
            pool.memset(half_neg[:], -0.5).then_inc(s_const, 1)
            pool.memset(ones[:], 1.0).then_inc(s_const, 1)
            pool.memset(unit[:], 1.0).then_inc(s_const, 1)
            pool.wait_ge(s_const, N_CONST)
            pool.affine_select(out=ident[:], in_=ident[:], compare_op=ALU.not_equal, fill=1.0, base=0,
                               pattern=[[-1, P]], channel_multiplier=1).then_inc(s_const, 1)
            for i in range(LEVELS):
                pool.memset(bound_b[:, i:i + 1], -level_bound(i) * STEEP).then_inc(s_const, 1)
            pool.memset(v_bd[:], 0.0).then_inc(s_const, 1)

            def body(n, proj, att, ln, between=lambda: None):
                if proj:
                    pool.wait_ge(s_xh, n + 1)
                    wait(pool, s_proj, 6 * n)
                    pool.tensor_tensor(x_l[:], xT[:], x_h[:].bitcast(F32), ALU.subtract).then_inc(s_xl, 1)
                    pool.wait_ge(s_nrec, n + 1)
                    wait(pool, s_ny, LEVELS * n)
                    pool.tensor_tensor(blocks_of(nf_w[:]), blocks_of(nf_raw[:]),
                                       nf_rec[:].unsqueeze(2).to_broadcast([P, QN, QBLOCK]), ALU.mult
                                       ).then_inc(s_nnorm, 1)
                if att:
                    pool.wait_ge(s_nacc, LEVELS * n)
                    v = blocks_of(nf_acc[:])
                    pool.tensor_tensor(v, v, nf_scale[:].unsqueeze(2).to_broadcast([P, QN, QBLOCK]), ALU.mult
                                       ).then_inc(s_ndq, 1)
                if proj:
                    wait(pool, s_ndq, n)
                    pool.tensor_tensor(nf_scale[:], nf_max[:], unit[:], ALU.mult).then_inc(s_nscale, 1)

                def rest(i):
                    v = qk[:, i].rearrange("p c t -> p (c t)")
                    pool.wait_ge(s_part_h, 2 * n + i + 1)
                    pool.tensor_tensor(v, v, qk_part[:, i, 0], ALU.subtract).then_inc(s_part_r, 1)

                def low(i):
                    pool.wait_ge(s_part_m, 2 * n + i + 1)
                    pool.tensor_tensor(qk_part[:, i, 2], qk[:, i].rearrange("p c t -> p (c t)"),
                                       qk_part[:, i, 1], ALU.subtract).then_inc(s_part_l, 1)

                if proj:
                    rest(0)
                    low(0)
                    rest(1)
                between()
                if ln:
                    pool.wait_ge(s_ld_ln, 32 * (n - 1))
                    pool.tensor_tensor(y1[:], y1[:], ctxT[:], ALU.add).then_inc(s_y, 1)
                if proj:
                    low(1)
                if ln:
                    pool.wait_ge(s_cen, n - 1)
                    pool.tensor_tensor(sq1[:], y1[:], y1[:], ALU.mult).then_inc(s_sq, 1)
                    pool.wait_ge(s_ve, n - 1)
                    pool.tensor_tensor(rstd1[:], ve1[:], half_neg[:], ALU.pow).then_inc(s_rstd, 1)
                    pool.wait_ge(s_rstd, n - 1)
                    pool.tensor_tensor(diag1[:], ident[:].unsqueeze(1).to_broadcast([P, NT, P]),
                                       rstd1[:].unsqueeze(2).to_broadcast([P, NT, P]), ALU.mult
                                       ).then_inc(s_diag, 1)

            def keep_scale_b(n):
                pool.wait_ge(s_bmax, n + 1)
                wait(pool, s_bdq, n)
                pool.tensor_tensor(nb_scale[:], nb_max[:], unit[:, 0:2 * N_B], ALU.mult).then_inc(s_bscale, 1)

            def dequantise_b(n):
                pool.wait_ge(s_bscale, n + 1)
                pool.wait_ge(s_bacc, LEVELS * (n + 1))
                v = blocks_of(slice_buffers(n)[1])
                pool.tensor_tensor(v, v, nb_scale[:].unsqueeze(2).to_broadcast([P, 2 * N_B, QBLOCK]), ALU.mult
                                   ).then_inc(s_bdq, 1)

            def low(half, n):
                nj = len(J_OF[half])
                done = len(J_OF[0]) * NB * half + nj * n
                for j in range(nj):
                    pool.wait_ge(s_hh, done + j + 1)
                    if j == 0:
                        wait(pool, s_down, NT * (NB * half + n))
                    pool.tensor_tensor(hid_l[:, j], hid[:, j % 2], hid_h[:, j].bitcast(F32), ALU.subtract
                                       ).then_inc(s_hl, 1)

            def split(half, n):
                before = len(J_OF[0]) * NB * half + len(J_OF[half]) * (n + 1)
                pool.wait_ge(s_x1h, NB * half + n + 2)
                wait(pool, s_gu, before)
                pool.tensor_tensor(x1_l[:], x1[:], x1_h[:].bitcast(F32), ALU.subtract).then_inc(s_x1l, 1)

            def rstd(n):
                for k in range(NT):
                    pool.wait_ge(s_ve2, NT * n + k + 1)
                    pool.tensor_tensor(rstd2[:, k:k + 1], ve2[:, k:k + 1], half_neg[:, 0:1], ALU.pow
                                       ).then_inc(s_rstd2, 1)

            def begin():
                keep_scale_b(0)
                split(0, -1)

            iterations(pool, body, begin)
            dequantise_b(0)
            def ffn(half, n, last=False):
                if not half and not last:
                    keep_scale_b(n + 1)
                low(half, n)
                if not (half and last):
                    split(half, n)
                if not half and not last:
                    dequantise_b(n + 1)
                if half:
                    rstd(n)

            ffn(0, 0)
            with pool.Fori(1, NB - 1) as n:
                ffn(0, n)
            ffn(0, NB - 1, last=True)
            ffn(1, 0)
            with pool.Fori(1, NB - 1) as n:
                ffn(1, n)
            ffn(1, NB - 1, last=True)

        @block.scalar
        def _(act):
            act.wait_ge(s_const, N_CONST + 1 + LEVELS)
            act.activation(ident_r[:], ident[:], ACT.Copy).then_inc(s_identr, 1)
            def cut_x(n):
                wait(act, s_st_xT, 16 * n)
                act.wait_ge(s_xtr, n + 1)
                act.activation(xT[:].rearrange("p c t -> p (c t)"), ps_t[:].rearrange("p a b -> p (a b)"),
                               ACT.Copy).then_inc(s_xT, 1)
                act.wait_ge(s_xT, n + 1)
                wait(act, s_proj, 6 * n)
                act.activation(x_h[:], xT[:], ACT.Copy).then_inc(s_xh, 1)

            for i in range(3 * KC):
                if i == 2 * KC:
                    cut_x(0)
                act.wait_ge(s_wtr, i + 1)
                act.activation(w_h[:, i // KC, i % KC], prep_bank(i), ACT.Copy).then_inc(s_wh, 1)
            act.wait_ge(s_bias, 48)

            def body(n, proj, att, ln, between=lambda: None):
                def steep(lo, hi, unit):
                    for i in range(lo, hi):
                        if i == 0:
                            act.wait_ge(s_nnorm, unit + 1)
                        at = LEVELS * unit + i
                        wait(act, s_nacc, at - NY + 1)
                        act.activation(nf_y[:, i % NY], nf_w[:], ACT.Identity,
                                       bias=bound_b[:, i:i + 1], scale=STEEP).then_inc(s_ny, 1)

                step = [0]

                def some(k):
                    hi = min(step[0] + k, LEVELS - LATE)
                    steep(step[0], hi, n)
                    step[0] = hi

                def exp(g):
                    if att:
                        act.wait_ge(s_ssub, NG * (n - 1) + g + 1)
                        act.activation(prob[:, g * GI:(g + 1) * GI], prob[:, g * GI:(g + 1) * GI], ACT.Exp,
                                       scale=1.0 / float(np.sqrt(np.float32(D)))).then_inc(s_exp, 1)

                if att:
                    steep(LEVELS - LATE, LEVELS - LATE + 1, n - 1)
                if proj and not first_block(n):
                    cut_x(n)
                if att:
                    steep(LEVELS - LATE + 1, LEVELS, n - 1)
                if proj:
                    some(1)
                if not proj:
                    for g in range(NG):
                        exp(g)
                if proj:
                    def middle(i):
                        act.wait_ge(s_part_r, 2 * n + i + 1)
                        act.activation(qk_part[:, i, 1], qk[:, i].rearrange("p c t -> p (c t)"), ACT.Copy
                                       ).then_inc(s_part_m, 1)

                    exp(0)
                    exp(1)
                    some(2)
                    for u in range(6):
                        i, half = divmod(u, 2)
                        act.wait_ge(s_proj, 6 * n + u + 1)
                        if u % 2 == 0:
                            if i < 2:
                                wait(act, s_part_l, 2 * (n - 1) + i + 1)
                            else:
                                wait(act, s_st_v, 16 * n)
                        for a in range(2):
                            c = 2 * half + a
                            dst = qk[:, i, c] if i < 2 else vT[:, c]
                            e = act.activation(dst, ps_a[:, u % 2, a * TB:a * TB + TB], ACT.Identity,
                                               bias=bias[:, i, c:c + 1])
                        e.then_inc(s_evac, 1)
                        if u in (1, 3):
                            act.wait_ge(s_evac, 6 * n + u + 1)
                            wait(act, (s_st_q, s_st_k)[i], 3 * 16 * n)
                            act.activation(qk_part[:, i, 0], qk[:, i].rearrange("p c t -> p (c t)"), ACT.Copy
                                           ).then_inc(s_part_h, 1)
                        if u in (1, 2):
                            exp(u + 1)
                        if u == 2:
                            middle(0)
                        if (u >= 3) == att or u == 5:
                            some(1)
                        if u == 4:
                            middle(1)
                for g in range(NG):
                    if att:
                        b = n - 1
                        act.wait_ge(s_pv, NG * b + g + 1)
                        if g == 0:
                            wait(act, s_st_ctx, 16 * Q4 * b)
                        act.activation(ctx[:, :, g * GI:(g + 1) * GI],
                                       ps_c[0:Q4 * D, g % 2].rearrange("p (i h) -> p h i", h=H),
                                       ACT.Copy).then_inc(s_ctx, 1)
                    if g == 1:
                        between()
                    if proj:
                        some(1)
                if proj:
                    some(LEVELS)

            prep_at = [0]

            def prepare(stages):
                lo = prep_at[0]
                prep_at[0] = hi = min(lo + stages, len(prep))
                for i in range(lo, hi):
                    w, j = prep[i]
                    act.wait_ge(s_ftr, i + 1)
                    src = prep_bank(i)
                    if w < 2:
                        dst, src = f1_h[:, w, :, j * P:(j + 1) * P], src.rearrange("p (c k) -> p c k", c=KC)
                    else:
                        dst = f3_h[:, j]
                    act.activation(dst, src, ACT.Copy).then_inc(s_fh, 1)

            step_b = [0]

            def steep_b(steps, n):
                w, _, y, ring = slice_buffers(n)
                for i in range(step_b[0], min(step_b[0] + steps, LEVELS)):
                    if i == 0:
                        act.wait_ge(s_bnorm, n + 1)
                    wait(act, s_bacc, LEVELS * n + i - ring + 1)
                    act.activation(y[:, i % ring], w, ACT.Identity,
                                   bias=bound_b[:, i:i + 1], scale=STEEP).then_inc(s_by, 1)
                step_b[0] = min(step_b[0] + steps, LEVELS)

            def split(block_n, done):
                act.wait_ge(s_x1ld, 16 * (block_n + 1))
                wait(act, s_gu, done)
                act.activation(x1_h[:], x1[:], ACT.Copy).then_inc(s_x1h, 1)

            def begin():
                prepare(3)
                split(0, 0)
                prepare(3 * JA - 3)
                steep_b(FIRST_B[0] + NYF, 0)

            iterations(act, body, begin)
            steep_b(LEVELS, 0)

            def ffn(half, n, last=False):
                nj, block_n = len(J_OF[half]), NB * half + n
                done = len(J_OF[0]) * NB * half + nj * n
                step_b[0] = 0

                def some(k):
                    if not half and not last:
                        steep_b(k, n + 1)

                def high(j):
                    act.wait_ge(s_hid, done + j + 1)
                    if j == 0:
                        wait(act, s_down, NT * block_n)
                    act.activation(hid_h[:, j], hid[:, j % 2], ACT.Copy).then_inc(s_hh, 1)

                for j in range(nj):
                    act.wait_ge(s_gu, done + j + 1)
                    wait(act, s_hl, done + j - 1)
                    wait(act, s_hh, done + j - 1)
                    act.activation(silu[:, j % 2], gu(j)[:, 0:TB], ACT.Silu).then_inc(s_silu, 1)
                    if j:
                        high(j - 1)
                        some(2)
                high(nj - 1)
                if not half and last:
                    prepare(3)
                if not (half and last):
                    split(block_n + 1, done + nj)
                some(LEVELS)
                for k in range(NT):
                    if half:
                        act.wait_ge(s_nmr2, NT * n + k + 1)
                        act.activation(o_tok[:, k], o_tok[:, k], ACT.Identity,
                                       bias=nmr2[:, k:k + 1], scale=rstd2[:, k:k + 1]).then_inc(s_o, 1)
                    else:
                        if isinstance(n, int) and NT * n + k == 0:
                            phase_1_over(act)
                        act.wait_ge(s_down, NT * n + k + 1)
                        act.activation(part[:, bass.ds(NT * n + k, 1), :].rearrange("p a e -> p (a e)"),
                                       ps_c[:, k], ACT.Copy).then_inc(s_part, 1)
                    if not half and last and k == 0:
                        prepare(4)

            ffn(0, 0)
            with act.Fori(1, NB - 1) as n:
                ffn(0, n)
            ffn(0, NB - 1, last=True)
            prepare(len(prep))
            with act.Fori(0, NB - 1) as n:
                ffn(1, n)
            ffn(1, NB - 1, last=True)

        @block.tensor
        def _(pe):
            def turn_x(n):
                pe.wait_ge(s_x, 16 * (n + 1))
                wait(pe, s_xT, n)
                for c in range(KC):
                    for k in range(NT):
                        t = pe.transpose(ps_t[:].rearrange("p a b -> p (a b)")[:, c * TB + k * P:c * TB + k * P + P],
                                         x_tok[:, k, c * P:(c + 1) * P], ident[:])
                t.then_inc(s_xtr, 1)

            pe.wait_ge(s_const, N_CONST + 1)
            for i in range(3):
                if i == 2:
                    turn_x(0)
                pe.wait_ge(s_wload[i], 16)
                for c in range(KC):
                    wait(pe, s_wl, i * KC + c - 3)
                    for m in range(KC):
                        t = pe.transpose(prep_bank(i * KC + c)[:, m * P:(m + 1) * P],
                                         wst[:, i % 2, m, c * P:(c + 1) * P], ident[:])
                    t.then_inc(s_wtr, 1)
            pe.wait_ge(s_wl, 3 * KC)
            pe.wait_ge(s_wh, 3 * KC)

            def three(dst, wh, wl, rh, rl, start, stop, skip=False):
                pe.matmul(dst, wh, rh, start=start, stop=False, skip_group_check=skip)
                pe.matmul(dst, wh, rl, start=False, stop=False, skip_group_check=skip)
                return pe.matmul(dst, wl, rh, start=False, stop=stop, skip_group_check=skip)

            def body(n, proj, att, ln, between=lambda: None):
                def scores(g):
                    b = n - 1
                    if not att:
                        return
                    wait(pe, s_ssub, NG * b + g - 1)
                    for i in range(GI):
                        for q in range(Q4):
                            s = q * TI + g * GI + i
                            t = pe.matmul(ps_s[32 * q:32 * q + 32, g % 2, i * H:(i + 1) * H],
                                          q_st[:, :, s], k_st[:, :, s], start=True, stop=True)
                    t.then_inc(s_score, 1)

                def project(u):
                    if not proj:
                        return
                    i, half = divmod(u, 2)
                    wait(pe, s_evac, 6 * n + u - 1)
                    for a in range(2):
                        m = 2 * half + a
                        for c in range(KC):
                            t = three(ps_a[:, u % 2, a * TB:a * TB + TB],
                                      w_h[:, i, c, m * P:(m + 1) * P], w_l[:, i, c, m * P:(m + 1) * P],
                                      x_h[:, c], x_l[:, c], c == 0, c == KC - 1)
                    t.then_inc(s_proj, 1)

                if proj and not first_block(n):
                    turn_x(n)
                if att:
                    pe.wait_ge(s_ld_stack, 16 * 12 * n)
                scores(0)
                scores(1)
                if proj:
                    pe.wait_ge(s_xh, n + 1)
                    pe.wait_ge(s_xl, n + 1)
                project(0)
                scores(2)
                project(1)
                scores(3)
                for u in (2, 3, 4, 5):
                    project(u)
                between()
                if ln:
                    pe.wait_ge(s_y, n - 1)
                    if proj:
                        pe.wait_ge(s_xT, n + 1)
                    for c in range(KC):
                        t = pe.matmul(ps_t[:, 0, 0:TB], mean_w[:], y1[:, c], start=(c == 0), stop=(c == KC - 1))
                    t.then_inc(s_mean, 1)
                if att:
                    b = n - 1
                    pe.wait_ge(s_ld_v, 16 * Q4 * (b + 1))
                    for g in range(NG):
                        pe.wait_ge(s_probT, NG * b + g + 1)
                        wait(pe, s_ctx, NG * b + g - 1)
                        for i in range(GI):
                            at = g * GI + i
                            t = pe.matmul(ps_c[0:Q4 * D, g % 2, i * H:(i + 1) * H],
                                          v_bd[:].rearrange("p a d i -> p (a d) i")[:, :, at],
                                          probT[:, at], start=True, stop=True)
                        t.then_inc(s_pv, 1)
                if ln:
                    pe.wait_ge(s_sq, n - 1)
                    for k in range(NT):
                        for c in range(KC):
                            t = pe.matmul(ps_t[:, 1, k:k + 1], sq1[:, c, k * P:(k + 1) * P], mean_w[:, 0:1],
                                          start=(c == 0), stop=(c == KC - 1))
                    t.then_inc(s_var, 1)
                    pe.wait_ge(s_diag, n - 1)
                    for k in range(NT):
                        t = pe.matmul(ps_t[:, 0, k * P:(k + 1) * P], ones[:], diag1[:, k], start=True, stop=True)
                    t.then_inc(s_spread, 1)
                    if att:
                        pe.wait_ge(s_x1, n - 1)

            prep_at = [0]

            def prepare(stages):
                lo = prep_at[0]
                prep_at[0] = hi = min(lo + stages, len(prep))
                for i in range(lo, hi):
                    pe.wait_ge(s_stg[prep_slot[i]], 16 * prep_count[i])
                    if i < 4:
                        pe.wait_ge(s_evac, 6 * NB)
                    elif i < 3 * JA or i >= 3 * JA + 4:
                        pe.wait_ge(s_fl, i - 3)
                    else:
                        pe.wait_ge(s_hid, JA * NB - (i < 3 * JA + 3))
                    for c in range(KC):
                        t = pe.transpose(prep_bank(i)[:, c * P:(c + 1) * P], stg[:, prep_slot[i], c], ident[:])
                    t.then_inc(s_ftr, 1)
                if hi in (3 * JA, len(prep)):
                    pe.wait_ge(s_fh, hi)
                    pe.wait_ge(s_fl, hi)

            iterations(pe, body, lambda: prepare(3 * JA))

            def ffn(half, n, last=False):
                nj, block_n = len(J_OF[half]), NB * half + n
                done = len(J_OF[0]) * NB * half + nj * n
                pe.wait_ge(s_x1h, block_n + 1)
                pe.wait_ge(s_x1l, block_n + 1)
                for j, chunk in enumerate(J_OF[half]):
                    cols = slice(chunk * P, (chunk + 1) * P)
                    wait(pe, s_hid, done + j - 3 if j > 3 else done)
                    for w in range(2):
                        for c in range(KC):
                            t = three(gu(j)[:, w * TB:(w + 1) * TB], f1_h[:, w, c, cols], f1_l[:, w, c, cols],
                                      x1_h[:, c], x1_l[:, c], c == 0, c == KC - 1)
                    t.then_inc(s_gu, 1)
                    if not half and j == nj // 2:
                        for k in range(NT):
                            wait(pe, s_part, NT * (n - 1) + k + 1)
                            for c in range(KC):
                                for x_part in (x1_h, x1_l):
                                    pe.matmul(ps_c[:, k, c * P:(c + 1) * P], x_part[:, c, k * P:(k + 1) * P],
                                              ident_r[:], start=(c == 0 and x_part is x1_h), stop=False,
                                              skip_group_check=True)
                if last:
                    prepare(3)
                def down(k, js):
                    for j in js:
                        if k == 0:
                            pe.wait_ge(s_hh, done + j + 1)
                            pe.wait_ge(s_hl, done + j + 1)
                        tok, chunk = slice(k * P, (k + 1) * P), J_OF[half][j]
                        t = three(ps_c[:, k], hid_h[:, j, tok], hid_l[:, j, tok], f3_h[:, chunk], f3_l[:, chunk],
                                  half == 1 and j == 0, j == nj - 1, skip=not half)
                    return t

                for k in range(NT):
                    if half:
                        wait(pe, s_sum, NT * (n - 1) + k + 1)
                    down(k, range(nj - 1))
                for k in range(NT):
                    down(k, [nj - 1]).then_inc(s_down, 1)
                    if last and k == 0:
                        prepare(4)

            pe.wait_ge(s_identr, 1)
            ffn(0, 0)
            with pe.Fori(1, NB - 1) as n:
                ffn(0, n)
            ffn(0, NB - 1, last=True)
            prepare(len(prep))
            pe.wait_ge(s_part, NT * NB)
            ffn(1, 0)
            with pe.Fori(1, NB) as n:
                ffn(1, n)

        @block.vector
        def _(dve):
            def scales(n):
                dve.wait_ge(s_nld, 3 * 16 * (n + 1))
                wait(dve, s_nscale, n)
                dve.tensor_reduce(nf_max[:], blocks_of(nf_raw[:]), AX.X, ALU.max, apply_absolute_value=True
                                  ).then_inc(s_nmax, 1)
                dve.wait_ge(s_nmax, n + 1)
                dve.tensor_scalar(nf_den[:], nf_max[:], TINY, None, ALU.max).then_inc(s_nden, 1)
                dve.wait_ge(s_nden, n + 1)
                wait(dve, s_nnorm, n)
                dve.reciprocal(nf_rec[:], nf_den[:]).then_inc(s_nrec, 1)

            for i in range(3 * KC):
                if i == 2 * KC:
                    scales(0)
                dve.wait_ge(s_wh, i + 1)
                dve.tensor_tensor(w_l[:, i // KC, i % KC], prep_bank(i), w_h[:, i // KC, i % KC].bitcast(F32),
                                  ALU.subtract).then_inc(s_wl, 1)

            def body(n, proj, att, ln, between=lambda: None):
                def lift(lo, hi, unit):
                    for i in range(lo, hi):
                        at = LEVELS * unit + i
                        y = nf_y[:, i % NY]
                        if i == 0:
                            wait(dve, s_nst, 3 * 16 * unit)
                        dve.wait_ge(s_ny, at + 1)
                        if i == 0:
                            dve.tensor_scalar(nf_acc[:], y, float(NF4[1]), float(NF4[0]), ALU.min, ALU.max
                                              ).then_inc(s_nacc, 1)
                        else:
                            dve.wait_ge(s_nacc, at)
                            dve.scalar_tensor_tensor(out=nf_acc[:], in0=y, scalar=float(NF4[i + 1]), in1=nf_acc[:],
                                                     op0=ALU.min, op1=ALU.max).then_inc(s_nacc, 1)

                step = [0]

                def some(k):
                    if proj:
                        hi = min(step[0] + k, LEVELS - LATE)
                        lift(step[0], hi, n)
                        step[0] = hi

                b = n - 1

                def part_of(t, g):
                    return t[:, g * GI:(g + 1) * GI]

                def wide(t, g):
                    return part_of(t, g).unsqueeze(2).to_broadcast([P, GI, H])

                def biggest(g):
                    dve.wait_ge(s_score, NG * b + g + 1)
                    dve.tensor_reduce(part_of(smax, g), scores_of(g), AX.X, ALU.max).then_inc(s_smax, 1)

                def scores_of(g):
                    return ps_s[:, g % 2].rearrange("p (i t) -> p i t", t=H)

                def shift(g):
                    dve.wait_ge(s_smax, NG * b + g + 1)
                    dve.tensor_tensor(part_of(prob, g), scores_of(g), wide(smax, g), ALU.subtract
                                      ).then_inc(s_ssub, 1)

                def total(g):
                    dve.wait_ge(s_exp, NG * b + g + 1)
                    dve.tensor_reduce(part_of(ssum, g), part_of(prob, g), AX.X, ALU.add).then_inc(s_ssum, 1)

                def invert(g):
                    dve.wait_ge(s_ssum, NG * b + g + 1)
                    dve.reciprocal(part_of(srec, g), part_of(ssum, g)).then_inc(s_srec, 1)

                def normalise(g):
                    dve.wait_ge(s_srec, NG * b + g + 1)
                    dve.tensor_tensor(part_of(prob, g), part_of(prob, g), wide(srec, g), ALU.mult
                                      ).then_inc(s_norm, 1)

                def turn(g):
                    dve.wait_ge(s_norm, NG * b + g + 1)
                    if g == 0:
                        wait(dve, s_pv, NG * b)
                    dve.transpose(part_of(probT, g).rearrange("p i h -> p (i h)"),
                                  part_of(prob, g).rearrange("p i h -> p (i h)")).then_inc(s_probT, 1)

                def softmax():
                    for step, g in ((biggest, 0), (biggest, 1), (shift, 0), (shift, 1),
                                    (total, 0), (biggest, 2), (invert, 0), (shift, 2), (normalise, 0),
                                    (total, 1), (turn, 0), (biggest, 3), (invert, 1), (shift, 3), (normalise, 1), (some, proj),
                                    (total, 2), (turn, 1), (invert, 2), (total, 3), (normalise, 2), (some, proj),
                                    (invert, 3), (turn, 2), (normalise, 3)):
                        step(g)
                    if proj:
                        some(1)
                    turn(3)

                if proj and not first_block(n):
                    scales(n)
                if att:
                    lift(LEVELS - LATE, LEVELS, n - 1)
                if att:
                    softmax()
                some(3)
                between()
                if ln:
                    dve.wait_ge(s_mean, n - 1)
                    dve.tensor_tensor(y1[:], y1[:], ps_t[:, 0, 0:TB].unsqueeze(1).to_broadcast([P, KC, TB]),
                                      ALU.subtract).then_inc(s_cen, 1)
                some(3)
                between()
                if ln:
                    dve.wait_ge(s_var, n - 1)
                    dve.tensor_scalar(ve1[:], ps_t[:, 1, 0:NT], EPS, None, ALU.add).then_inc(s_ve, 1)
                some(1)
                between()
                if ln:
                    dve.wait_ge(s_spread, n - 1)
                    dve.tensor_tensor(y1[:], y1[:], ps_t[:, 0, 0:TB].unsqueeze(1).to_broadcast([P, KC, TB]),
                                      ALU.mult).then_inc(s_x1, 1)
                some(LEVELS)

            prep_at = [0]

            def prepare(stages):
                lo = prep_at[0]
                prep_at[0] = hi = min(lo + stages, len(prep))
                for i in range(lo, hi):
                    w, j = prep[i]
                    dve.wait_ge(s_fh, i + 1)
                    src = prep_bank(i)
                    if w < 2:
                        at = (slice(None), w, slice(None), slice(j * P, (j + 1) * P))
                        hi, lo = f1_h[at], f1_l[at]
                        src = src.rearrange("p (c k) -> p c k", c=KC)
                    else:
                        hi, lo = f3_h[:, j], f3_l[:, j]
                    dve.tensor_tensor(lo, src, hi.bitcast(F32), ALU.subtract).then_inc(s_fl, 1)

            def scales_b(n):
                dve.wait_ge(s_bld, 2 * 16 * (n + 1))
                wait(dve, s_bscale, n)
                dve.tensor_reduce(nb_max[:], blocks_of(slice_buffers(n)[0]), AX.X, ALU.max,
                                  apply_absolute_value=True).then_inc(s_bmax, 1)
                dve.wait_ge(s_bmax, n + 1)
                dve.tensor_scalar(nb_den[:], nb_max[:], TINY, None, ALU.max).then_inc(s_bden, 1)
                dve.wait_ge(s_bden, n + 1)
                dve.reciprocal(nb_rec[:], nb_den[:]).then_inc(s_brec, 1)
                dve.wait_ge(s_brec, n + 1)
                v = blocks_of(slice_buffers(n)[0])
                dve.tensor_tensor(v, v, nb_rec[:].unsqueeze(2).to_broadcast([P, 2 * N_B, QBLOCK]), ALU.mult
                                  ).then_inc(s_bnorm, 1)

            step_b = [0]

            def lift_b(steps, n):
                _, acc, y, ring = slice_buffers(n)
                for i in range(step_b[0], min(step_b[0] + steps, LEVELS)):
                    if i == 0:
                        wait(dve, s_bst, 2 * 16 * n)
                    dve.wait_ge(s_by, LEVELS * n + i + 1)
                    if i == 0:
                        dve.tensor_scalar(acc, y[:, 0], float(NF4[1]), float(NF4[0]), ALU.min, ALU.max
                                          ).then_inc(s_bacc, 1)
                    else:
                        dve.wait_ge(s_bacc, LEVELS * n + i)
                        dve.scalar_tensor_tensor(out=acc, in0=y[:, i % ring], scalar=float(NF4[i + 1]), in1=acc,
                                                 op0=ALU.min, op1=ALU.max).then_inc(s_bacc, 1)
                step_b[0] = min(step_b[0] + steps, LEVELS)

            turns = iter(FIRST_B)

            def between():
                if prep_at[0] == 0:
                    scales_b(0)
                    prepare(3 * JA)
                lift_b(next(turns), 0)

            iterations(dve, body, between)

            def ffn(half, n, last=False):
                nj, block_n = len(J_OF[half]), NB * half + n
                done = len(J_OF[0]) * NB * half + nj * n
                step_b[0] = 0

                def some(k):
                    if not half and not last:
                        lift_b(k, n + 1)

                for j in range(nj):
                    dve.wait_ge(s_silu, done + j + 1)
                    dve.tensor_tensor(hid[:, j % 2], silu[:, j % 2], gu(j)[:, TB:2 * TB], ALU.mult
                                      ).then_inc(s_hid, 1)
                    if j == 0 and not half and not last:
                        scales_b(n + 1)
                    if j:
                        some(2)
                    if j == 1 and last and not half:
                        dve.wait_ge(s_bst, 2 * 16 * NB)
                        dve.memset(stg[:, NS], 0.0).then_inc(s_pad, 1)
                if not half and last:
                    prepare(7)
                some(LEVELS)
                if not half:
                    return
                for k in range(NT):
                    at = NT * n + k + 1
                    dve.wait_ge(s_down, NT * NB + at)
                    wait(dve, s_out[k], 16 * n)
                    dve.tensor_tensor(o_tok[:, k], ps_c[:, k],
                                      part[:, bass.ds(NT * n + k, 1), :].rearrange("p a e -> p (a e)"), ALU.add
                                      ).then_inc(s_sum, 1)
                    dve.wait_ge(s_sum, at)
                    dve.bn_stats(st6[:, k], o_tok[:, k]).then_inc(s_bn, 1)
                    hold(dve, s_bn, at)
                    dve.bn_aggr(mv[:, k], st6[:, k]).then_inc(s_mv, 1)
                    dve.wait_ge(s_mv, at)
                    dve.tensor_scalar(ve2[:, k:k + 1], mv[:, k, 1:2], EPS, None, ALU.add).then_inc(s_ve2, 1)
                    dve.wait_ge(s_rstd2, at)
                    wait(dve, s_o, at - NT)
                    dve.scalar_tensor_tensor(out=nmr2[:, k:k + 1], in0=mv[:, k, 0:1], scalar=-1.0,
                                             in1=rstd2[:, k:k + 1], op0=ALU.mult, op1=ALU.mult
                                             ).then_inc(s_nmr2, 1)

            ffn(0, 0)
            with dve.Fori(1, NB - 1) as n:
                ffn(0, n)
            ffn(0, NB - 1, last=True)
            prepare(len(prep))
            ffn(1, 0)
            with dve.Fori(1, NB - 1) as n:
                ffn(1, n)
            ffn(1, NB - 1, last=True)


_INS = ["L0_attn_hidden_states", "L0_attn_wq", "L0_attn_bq", "L0_attn_wk", "L0_attn_bk", "L0_attn_wv",
        "L0_attn_bv", "L0_ffn_w1", "L0_ffn_w2", "L0_ffn_w3"]


def kernel(**inputs):
    import concourse.bacc as _bacc
    from concourse.bass_utils import run_bass_kernel_spmd as _run

    nc = _bacc.Bacc("TRN2", target_bir_lowering=False, num_devices=1)
    arrays, args = {}, []
    for name in _INS:
        a = np.ascontiguousarray(inputs[name])
        arrays[f"in_{name}"] = a
        args.append(nc.dram_tensor(f"in_{name}", a.shape, mybir.dt.from_np(a.dtype), kind="ExternalInput").ap())
    shape = inputs["L0_attn_hidden_states"].shape
    args.append(nc.dram_tensor("out_0", shape, F32, kind="ExternalOutput").ap())
    layer_kernel(nc, *args)
    r = _run(nc, [arrays], core_ids=[0])
    return r.results[0]["out_0"]
```
